# Optimizing a Trainium2 kernel written in Bass

```python
import numpy as np
import jax
import jax.numpy as jnp

def _softmax(x, axis=-1):
    return jax.nn.softmax(x, axis=axis)
def _gelu(x):
    return jax.nn.gelu(x, approximate=True)
def _silu(x):
    return jax.nn.silu(x)
def _sigmoid(x):
    return jax.nn.sigmoid(x)
def _layernorm(x, axis=-1, eps=1e-5):
    m = jnp.mean(x, axis=axis, keepdims=True)
    v = jnp.var(x, axis=axis, keepdims=True)
    return (x - m) / jnp.sqrt(v + eps)
def _scatter_add(tgt, idx, src, axis=0):
    return tgt.at[idx].add(src)
def _segment_sum(src, seg, n):
    return jax.ops.segment_sum(src, seg, n)

kernel_name = 'mk_conv_preact_d2_conv_nchw256_b7780a'

def setup_inputs(seed: int = 0):
    np.random.seed(seed)
    _w = jnp.asarray
    def _rec_inputs():
        import jax
        import jax.numpy as jnp
        _gk = jax.random.key(seed)
        x = -0.000125 + 0.9999 * jax.random.normal(jax.random.fold_in(_gk, 1), (8, 256, 128, 128), jnp.float32)
        return x
    x = _rec_inputs()
    def _L0_conv_setup():
        import jax, jax.numpy as jnp
        import numpy as np
        FEAT, HEADS, GROUPS = (256, 8, 4)
        HD = FEAT // HEADS

        def conv2d(x, w, b, pad):
            y = jax.lax.conv_general_dilated(x, w, (1, 1), [(pad, pad), (pad, pad)], dimension_numbers=('NCHW', 'OIHW', 'NCHW'))
            return y + b[None, :, None, None]

        def _sample_one(img, grid):
            C, H, W = img.shape
            ix = ((grid[..., 0] + 1.0) * W - 1.0) * 0.5
            iy = ((grid[..., 1] + 1.0) * H - 1.0) * 0.5
            x0 = jnp.floor(ix)
            y0 = jnp.floor(iy)
            x1 = x0 + 1.0
            y1 = y0 + 1.0
            w00 = (x1 - ix) * (y1 - iy)
            w01 = (ix - x0) * (y1 - iy)
            w10 = (x1 - ix) * (iy - y0)
            w11 = (ix - x0) * (iy - y0)

            def g(xq, yq, w):
                valid = (xq >= 0) & (xq <= W - 1) & (yq >= 0) & (yq <= H - 1)
                xc = jnp.clip(xq, 0, W - 1).astype(jnp.int32)
                yc = jnp.clip(yq, 0, H - 1).astype(jnp.int32)
                return img[:, yc, xc] * (w * valid)[None]
            return g(x0, y0, w00) + g(x1, y0, w01) + g(x0, y1, w10) + g(x1, y1, w11)
        _sample = jax.vmap(jax.vmap(_sample_one))
        key = jax.random.key(seed)
        ks = jax.random.split(key, 8)
        B, C, H, W = (8, FEAT, 128, 128)
        x = jax.random.normal(ks[0], (B, C, H, W), jnp.float32)
        offset_w = 0.01 * jax.random.normal(ks[1], (2 * GROUPS, C, 3, 3), jnp.float32)
        offset_b = jnp.zeros((2 * GROUPS,), jnp.float32)
        mod_w = 0.01 * jax.random.normal(ks[2], (GROUPS, C, 3, 3), jnp.float32)
        mod_b = jnp.ones((GROUPS,), jnp.float32)
        kv_w = 0.02 * jax.random.normal(ks[3], (2 * C, C, 1, 1), jnp.float32)
        kv_b = jnp.zeros((2 * C,), jnp.float32)
        out_w = 0.02 * jax.random.normal(ks[4], (C, C, 1, 1), jnp.float32)
        out_b = jnp.zeros((C,), jnp.float32)
        return dict(x=x, offset_w=offset_w, offset_b=offset_b, mod_w=mod_w, mod_b=mod_b, kv_w=kv_w, kv_b=kv_b, out_w=out_w, out_b=out_b)
    _L0_conv_all = _L0_conv_setup()
    _L0_conv_in = {k: v for k, v in _L0_conv_all.items() if k in ('offset_w', 'offset_b', 'mod_w', 'mod_b', 'kv_w', 'kv_b', 'out_w', 'out_b', )}
    del _L0_conv_all

    def _L1_conv_setup():
        import jax, jax.numpy as jnp
        import numpy as np
        EPS = 0.0001

        def _zca_forward(x, weight, bias, groups=16):
            N, C, H, W = x.shape
            G = groups
            c = C // G
            M = N * H * W
            xf = jnp.transpose(x, (1, 0, 2, 3)).reshape(C, M)
            mu = jnp.mean(xf, axis=1, keepdims=True)
            xc = xf - mu
            xg = xc.reshape(G, c, M)
            cov = jnp.einsum('gim,gjm->gij', xg, xg) / M
            cov = cov + EPS * jnp.eye(c, dtype=x.dtype)
            e, v = jnp.linalg.eigh(cov)
            inv_sqrt = jax.lax.rsqrt(e)
            proj = jnp.einsum('gik,gk,gjk->gij', v, inv_sqrt, v)
            xw = jnp.einsum('gij,gjm->gim', proj, xg).reshape(C, M)
            out = xw * weight + bias
            return jnp.transpose(out.reshape(C, N, H, W), (1, 0, 2, 3))
        key = jax.random.key(seed)
        k1, k2 = jax.random.split(key)
        N, C, H, W = (64, 256, 56, 56)
        x = jax.random.normal(k1, (N, C, H, W), dtype=jnp.float32)
        weight = jax.random.uniform(k2, (C, 1), dtype=jnp.float32)
        bias = jnp.zeros((C, 1), dtype=jnp.float32)
        return {'x': x, 'weight': weight, 'bias': bias}
    _L1_conv_all = _L1_conv_setup()
    _L1_conv_in = {k: v for k, v in _L1_conv_all.items() if k in ('weight', 'bias', )}
    del _L1_conv_all

    return {
        "x": x,
        "L0_conv_offset_w": _L0_conv_in["offset_w"],
        "L0_conv_offset_b": _L0_conv_in["offset_b"],
        "L0_conv_mod_w": _L0_conv_in["mod_w"],
        "L0_conv_mod_b": _L0_conv_in["mod_b"],
        "L0_conv_kv_w": _L0_conv_in["kv_w"],
        "L0_conv_kv_b": _L0_conv_in["kv_b"],
        "L0_conv_out_w": _L0_conv_in["out_w"],
        "L0_conv_out_b": _L0_conv_in["out_b"],
        "L1_conv_weight": _L1_conv_in["weight"],
        "L1_conv_bias": _L1_conv_in["bias"],
    }

def reference(x, L0_conv_offset_w, L0_conv_offset_b, L0_conv_mod_w, L0_conv_mod_b, L0_conv_kv_w, L0_conv_kv_b, L0_conv_out_w, L0_conv_out_b, L1_conv_weight, L1_conv_bias):
    import jax
    import jax.numpy as jnp
    def _L0_conv_ref(x, offset_w, offset_b, mod_w, mod_b, kv_w, kv_b, out_w, out_b):
        import jax, jax.numpy as jnp
        import numpy as np
        FEAT, HEADS, GROUPS = (256, 8, 4)
        HD = FEAT // HEADS

        def conv2d(x, w, b, pad):
            y = jax.lax.conv_general_dilated(x, w, (1, 1), [(pad, pad), (pad, pad)], dimension_numbers=('NCHW', 'OIHW', 'NCHW'))
            return y + b[None, :, None, None]

        def _sample_one(img, grid):
            C, H, W = img.shape
            ix = ((grid[..., 0] + 1.0) * W - 1.0) * 0.5
            iy = ((grid[..., 1] + 1.0) * H - 1.0) * 0.5
            x0 = jnp.floor(ix)
            y0 = jnp.floor(iy)
            x1 = x0 + 1.0
            y1 = y0 + 1.0
            w00 = (x1 - ix) * (y1 - iy)
            w01 = (ix - x0) * (y1 - iy)
            w10 = (x1 - ix) * (iy - y0)
            w11 = (ix - x0) * (iy - y0)

            def g(xq, yq, w):
                valid = (xq >= 0) & (xq <= W - 1) & (yq >= 0) & (yq <= H - 1)
                xc = jnp.clip(xq, 0, W - 1).astype(jnp.int32)
                yc = jnp.clip(yq, 0, H - 1).astype(jnp.int32)
                return img[:, yc, xc] * (w * valid)[None]
            return g(x0, y0, w00) + g(x1, y0, w01) + g(x0, y1, w10) + g(x1, y1, w11)
        _sample = jax.vmap(jax.vmap(_sample_one))
        B, C, H, W = x.shape
        offsets = conv2d(x, offset_w, offset_b, 1)
        mod = 1.0 + jnp.tanh(conv2d(x, mod_w, mod_b, 1))
        kv = conv2d(x, kv_w, kv_b, 0)
        v = kv[:, C:].reshape(B, HEADS, HD, H, W)
        g_idx = jnp.arange(HEADS) % GROUPS
        off = offsets.reshape(B, GROUPS, 2, H, W)[:, g_idx]
        xx = jnp.arange(W, dtype=x.dtype)[None, :]
        yy = jnp.arange(H, dtype=x.dtype)[:, None]
        px = xx + off[:, :, 0]
        py = yy + off[:, :, 1]
        gx = 2.0 * px / (W - 1) - 1.0
        gy = 2.0 * py / (H - 1) - 1.0
        grid = jnp.stack([gx, gy], axis=-1)
        sampled = _sample(v, grid) * mod[:, g_idx][:, :, None]
        out = sampled.reshape(B, C, H, W)
        return conv2d(out, out_w, out_b, 0)

    def _L1_conv_ref(x, weight, bias):
        import jax, jax.numpy as jnp
        import numpy as np
        EPS = 0.0001

        def _zca_forward(x, weight, bias, groups=16):
            N, C, H, W = x.shape
            G = groups
            c = C // G
            M = N * H * W
            xf = jnp.transpose(x, (1, 0, 2, 3)).reshape(C, M)
            mu = jnp.mean(xf, axis=1, keepdims=True)
            xc = xf - mu
            xg = xc.reshape(G, c, M)
            cov = jnp.einsum('gim,gjm->gij', xg, xg) / M
            cov = cov + EPS * jnp.eye(c, dtype=x.dtype)
            e, v = jnp.linalg.eigh(cov)
            inv_sqrt = jax.lax.rsqrt(e)
            proj = jnp.einsum('gik,gk,gjk->gij', v, inv_sqrt, v)
            xw = jnp.einsum('gij,gjm->gim', proj, xg).reshape(C, M)
            out = xw * weight + bias
            return jnp.transpose(out.reshape(C, N, H, W), (1, 0, 2, 3))
        return _zca_forward(x, weight, bias)

    def _gn(v, G=32, eps=1e-5):
        B_, C_, H_, W_ = v.shape
        g = v.reshape(B_, G, C_ // G, H_, W_)
        m = jnp.mean(g, axis=(2, 3, 4), keepdims=True)
        s = jnp.var(g, axis=(2, 3, 4), keepdims=True)
        return ((g - m) / jnp.sqrt(s + eps)).reshape(v.shape)

    def _ln_c(v, eps=1e-6):
        m = jnp.mean(v, axis=1, keepdims=True)
        s = jnp.var(v, axis=1, keepdims=True)
        return (v - m) / jnp.sqrt(s + eps)

    def _ln_t(v, eps=1e-5):
        m = jnp.mean(v, axis=-1, keepdims=True)
        s = jnp.var(v, axis=-1, keepdims=True)
        return (v - m) / jnp.sqrt(s + eps)

    def _to_tokens(v):
        B_, C_, H_, W_ = v.shape
        return v.reshape(B_, C_, H_ * W_).transpose(0, 2, 1)
    def _from_tokens(t, like):
        B_, C_, H_, W_ = like.shape
        return t.transpose(0, 2, 1).reshape(B_, C_, H_, W_)

    x = x + _L0_conv_ref(_gn(x), L0_conv_offset_w, L0_conv_offset_b, L0_conv_mod_w, L0_conv_mod_b, L0_conv_kv_w, L0_conv_kv_b, L0_conv_out_w, L0_conv_out_b)
    x = x + _L1_conv_ref(_gn(x), L1_conv_weight, L1_conv_bias)
    return x


_drawn_inputs = setup_inputs


def setup_inputs(seed=0):
    import zlib

    import numpy as np

    out = dict(_drawn_inputs(seed))
    spreads = {'L0_conv_offset_b': (0.0, 0.368),
     'L0_conv_mod_b': (1.0, 0.6),
     'L0_conv_kv_b': (0.0, 0.1),
     'L0_conv_out_b': (0.0, 0.1),
     'L1_conv_bias': (0.0, 0.1)}
    factors = {'L0_conv_mod_w': 3.19}
    for name, (base, spread) in spreads.items():
        noise = np.random.default_rng([zlib.crc32(name.encode()), seed]).standard_normal(out[name].shape)
        drawn = base * np.exp(spread * noise) if base else spread * noise
        out[name] = jnp.asarray(drawn.astype(out[name].dtype))
    for name, factor in factors.items():
        out[name] = (out[name] * factor).astype(out[name].dtype)
    return out
```

```python
from contextlib import ExitStack

import concourse.bass as bass
from concourse import mybir

ALU = mybir.AluOpType
ACT = mybir.ActivationFunctionType
AX_X = mybir.AxisListType.X
F32 = mybir.dt.float32
U32 = mybir.dt.uint32

P = 128
C, H, W = 256, 128, 128
PIX = H * W
CC = C // P
G = 4
CG = C // G
NTAP = 9
NO = 3 * G
NT = NTAP * NO
NA = C + NT
ROWS = 4
BP = ROWS * W
BLOCKS = H // ROWS
PAIRS = BLOCKS // 2
NJ = ROWS * G
PATCH = 4 * CG
ENT = 2 * CG
VROWS = H
VROW = G * W * ENT
IMG = VROWS * VROW
SR = 16
SBLK = H // SR
QR = 32
NQ = H // QR
GN1 = 8
GZ = 16
EPS_GN, EPS_Z = 1e-5, 1e-4
MAGIC = 12582912.0
STEPS = 24


def deform_zca_kernel(nc, B, x, wA, biasA, bias_off, wO, bias_o, w_z, bias_z, out):
    v2 = [nc.dram_tensor(f"v2_{j}", [IMG], F32, kind="Internal").ap() for j in range(2)]
    x1 = nc.dram_tensor("x1", [B, CC, P, PIX], F32, kind="Internal").ap()
    x_v = x.rearrange("b (c p) h w -> b p c (h w)", p=P)
    out_v = out.rearrange("b (c p) h w -> b p c (h w)", p=P)
    x1_v = x1.rearrange("b c p n -> b p c n")
    v2_flat = [v.rearrange("(a n) -> a n", a=1) for v in v2]
    v2_rows = [v.rearrange("(r x e) -> x r e", x=W, e=ENT) for v in v2]

    ctx = ExitStack()
    with ctx:
        def sb(name, shape, dt=F32):
            return ctx.enter_context(nc.sbuf_tensor(name, shape, dt))

        def ps(name):
            return ctx.enter_context(nc.psum_tensor(name, [P, 512], F32))

        def sem(name):
            return ctx.enter_context(nc.semaphore(name))

        ident = sb("ident", [P, P])
        shift = sb("shift", [P, 3, P])
        avg8 = sb("avg8", [P, P])
        same16 = sb("same16", [P, P])
        wA_sb = sb("wA_sb", [P, CC, NA])
        wO_sb = sb("wO_sb", [P, CC, C])
        biasA_sb = sb("biasA_sb", [P, NA])
        off_b = sb("off_b", [P, NO])
        bo_sb = sb("bo_sb", [P, CC])
        wz_sb = sb("wz_sb", [P, CC])
        bz_sb = sb("bz_sb", [P, CC])
        grid = sb("grid", [P, H, 2 * G])
        first_patch = sb("first_patch", [P, QR, G])
        opening = sb("opening", [P, 8, CC])
        wB = sb("wB", [P, CC, NA])
        mean_bc = sb("mean_bc", [P, CC, P])
        biasB = sb("biasB", [P, NA])
        taps = sb("taps", [P, H + 2, NT])
        index = sb("index", [P, H * G], U32)
        weight = sb("weight", [P, H * G * 4])
        xa = [sb(f"xa{j}", [P, CC, BP]) for j in range(2)]
        vring = [sb(f"vring{j}", [P, ROWS, G, 2, CG]) for j in range(2)]
        index_now = [sb(f"index_now{j}", [P, NJ], U32) for j in range(2)]
        patch = [sb(f"patch{j}", [P, NJ, PATCH]) for j in range(2)]
        samp = [sb(f"samp{j}", [P, ROWS, C]) for j in range(2)]
        sampT = sb("sampT", [P, CC, BP])
        xr = [sb(f"xr{j}", [P, CC, BP]) for j in range(2)]
        x1T = sb("x1T", [P, ROWS, CC, P + 1])
        gram = sb("gram", [P, B, CC, P + 1])
        bst = sb("bst", [P, CC, PIX // 512, 6])
        mv = sb("mv", [P, CC, B, 2])
        mv_now = sb("mv_now", [P, CC, 2])
        mean_x = sb("mean_x", [P, CC, B])
        rstd_x = sb("rstd_x", [P, CC, B])
        pt = {n: sb("p_" + n, [P, QR, 2 * G]) for n in ("ix", "a", "b", "m0", "m1")}
        pm = {n: sb("p_" + n, [P, QR, G]) for n in ("tm", "th", "w0", "w1", "ia")}

        psA = [ps(f"psA{i}") for i in range(2)]
        psI = ps("psI")
        psT = [ps(f"psT{i}") for i in range(2)]
        psO = [ps(f"psO{i}") for i in range(2)]
        psG = ps("psG")

        const_ld = sem("const_ld")
        consts = sem("consts")
        zeros = sem("zeros")
        passed = sem("passed")
        setup_v = sem("setup_v")
        st_ld = [sem(f"st_ld{j}") for j in range(2)]
        st_used = [sem(f"st_used{j}") for j in range(2)]
        st_v = sem("st_v")
        st_p = sem("st_p")
        st_a = sem("st_a")
        xa_ld = [sem(f"xa_ld{j}") for j in range(2)]
        row_full = [[sem(f"row_full{j}{r}") for r in range(ROWS)] for j in range(2)]
        psA_free = [sem(f"psA_free{j}") for j in range(2)]
        v_row = sem("v_row")
        v_dup = sem("v_dup")
        v_st = [sem(f"v_st{j}") for j in range(2)]
        w_ready = sem("w_ready")
        psI_full = sem("psI_full")
        psI_free = sem("psI_free")
        place_v = sem("place_v")
        mod_in = sem("mod_in")
        mod_out = sem("mod_out")
        placed = sem("placed")
        index_cp = sem("index_cp")
        got = [[sem(f"got{j}{h}") for h in range(2)] for j in range(2)]
        weighted = sem("weighted")
        halved = sem("halved")
        sampled = [sem(f"sampled{j}") for j in range(2)]
        psT_full = [sem(f"psT_full{j}") for j in range(2)]
        psT_free = [sem(f"psT_free{j}") for j in range(2)]
        psO_full = [sem(f"psO_full{j}") for j in range(2)]
        psO_free = [sem(f"psO_free{j}") for j in range(2)]
        xr_ld = [sem(f"xr_ld{j}") for j in range(2)]
        x1_st = [sem(f"x1_st{j}") for j in range(2)]
        psG_full = [sem(f"psG_full{j}") for j in range(2)]
        psG_free = sem("psG_free")
        wh_v = sem("wh_v")
        wh_p = sem("wh_p")
        wh_a = sem("wh_a")
        ns_t = sem("ns_t")
        ns_zy = sem("ns_zy")
        ns_zt = sem("ns_zt")
        ns_new = sem("ns_new")
        map_v = sem("map_v")
        y_ld = [sem(f"y_ld{j}") for j in range(4)]
        y_mm = [sem(f"y_mm{j}") for j in range(4)]
        y_add = [sem(f"y_add{j}") for j in range(4)]
        y_st = [sem(f"y_st{j}") for j in range(4)]

        wk = patch[0][:, :, :].rearrange("p j e -> p (j e)")
        wk2 = patch[1][:, :, :].rearrange("p j e -> p (j e)")

        def area(base, at, n):
            return base[:, at:at + n]

        def alone(eng):
            eng.sem_inc(passed, 1)

        def images(eng, first, last, body):
            if last - first >= 2:
                with eng.Fori(0, (last - first) // 2) as h:
                    for k in range(2):
                        body(h * 2 + (first + k), (first + k) % 2)
            if (last - first) % 2:
                body(last - 1, (last - 1) % 2)

        block = ctx.enter_context(nc.Block())

        gm = area(wk, 0, CC * B).rearrange("p (c b) -> p c b", b=B)
        rs = area(wk, 16, CC * B).rearrange("p (c b) -> p c b", b=B)
        sums = area(wk, 32, CC * B).rearrange("p (c b) -> p c b", b=B)
        st2 = area(wk, 48, CC * B * 2).rearrange("p (c b k) -> p c b k", b=B, k=2)
        g_b = area(wk, 80, CC * B).rearrange("p (c b) -> p c b", b=B)
        a_b = area(wk, 96, CC * B).rearrange("p (c b) -> p c b", b=B)
        d_b = area(wk, 112, CC * B).rearrange("p (c b) -> p c b", b=B)
        mu = area(wk, 128, CC)
        gmu = area(wk, 136, CC * B).rearrange("p (c b) -> p c b", b=B)
        cst = area(wk, 152, CC * B).rearrange("p (c b) -> p c b", b=B)
        tr = area(wk, 168, CC)
        rtr = area(wk, 172, CC)
        srt = area(wk, 176, CC)
        var = area(wk, 184, CC * B).rearrange("p (c b) -> p c b", b=B)
        scr = area(wk, 256, CC * B * P).rearrange("p (c b n) -> p c b n", b=B, n=P)
        cov = area(wk2, 0, CC * P).rearrange("p (c n) -> p c n", n=P)
        Y = area(wk2, 256, CC * P).rearrange("p (c n) -> p c n", n=P)
        Z = area(wk2, 512, CC * P).rearrange("p (c n) -> p c n", n=P)
        T = area(wk2, 768, CC * P).rearrange("p (c n) -> p c n", n=P)
        rowsT = area(wk2, 1024, CC * 4 * P).rearrange("p (c k n) -> p c k n", k=4, n=P)
        dg = area(wk2, 2048, CC * P).rearrange("p (c n) -> p c n", n=P)
        pw = area(wk2, 2304, CC * P).rearrange("p (c n) -> p c n", n=P)
        amap = area(wk2, 2560, CC * P).rearrange("p (c n) -> p c n", n=P)
        i15 = area(wk2, 2816, P)
        cnow = area(wk2, 2944, CC)
        y_buf = (xr[0], xr[1], xa[0], xa[1])
        y_bank = (psO, psA, psT, (psI, psG))
        mark = {}


        P_STATS = 1
        P_ROWS = P_STATS + 1
        P_GRAM = P_ROWS + CC
        P_CROSS = P_GRAM + CC * B
        P_TRACE = P_CROSS + CC
        P_PW = P_TRACE + 1
        P_CST = P_PW + CC

        @block.sync
        def _(eng):
            for dst, src in ((wA_sb[:, :, :], wA.rearrange("(c p) n -> p c n", p=P)),
                             (wO_sb[:, :, :], wO.rearrange("(c p) n -> p c n", p=P)),
                             (biasA_sb[:, :], biasA.partition_broadcast(P)),
                             (off_b[:, :], bias_off.partition_broadcast(P)),
                             (bo_sb[:, :], bias_o), (wz_sb[:, :], w_z), (bz_sb[:, :], bias_z)):
                eng.dma_start(dst, src).then_inc(const_ld, 16)
            for n, store in enumerate((*v_st, *x1_st, *y_st)):
                eng.dma_start(opening[:, n, :], bias_o).then_inc(store, 16)
            with eng.Fori(0, B) as b:
                with eng.Fori(0, SBLK // 2) as i:
                    for j in range(2):
                        use = eng.snap(b * (SBLK // 2) + i)
                        at = eng.snap((i * 2 + j) * (SR * W))
                        eng.wait_ge(st_used[j], use + 1)
                        alone(eng)
                        eng.dma_start(patch[j][:, :, :].rearrange("p j e -> p (j e)")
                                      .rearrange("p (c n) -> p c n", c=CC),
                                      x_v[bass.ds(b, 1), :, :, bass.ds(at, SR * W)]
                                      .rearrange("a p c n -> (a p) c n")).then_inc(st_ld[j], 16)

            def load_a(b, i, j):
                p = eng.snap(b * PAIRS + i)
                at = eng.snap((i * 2 + j) * BP)
                bb = eng.snap(b) if not isinstance(b, int) else b
                eng.wait_ge(row_full[j][ROWS - 1], p + 1)
                alone(eng)
                eng.dma_start(xa[j][:, :, :], x_v[bass.ds(bb, 1), :, :, bass.ds(at, BP)]
                              .rearrange("a p c n -> (a p) c n")).then_inc(xa_ld[j], 16)

            def load_r(b, i, j):
                p = eng.snap(b * PAIRS + i)
                p16 = eng.snap((b * PAIRS + i) * 16)
                at = eng.snap((i * 2 + j) * BP)
                bb = eng.snap(b) if not isinstance(b, int) else b
                eng.wait_ge(psG_full[j], p + 1)
                alone(eng)
                eng.wait_ge(x1_st[j], p16 + 16)
                alone(eng)
                eng.dma_start(xr[j][:, :, :], x_v[bass.ds(bb, 1), :, :, bass.ds(at, BP)]
                              .rearrange("a p c n -> (a p) c n")).then_inc(xr_ld[j], 16)

            with eng.Fori(0, PAIRS) as i:
                for j in range(2):
                    load_a(0, i, j)
            with eng.Fori(0, B - 1) as b:
                with eng.Fori(0, PAIRS) as i:
                    for j in range(2):
                        load_a(b + 1, i, j)
                        load_r(b, i, j)
            with eng.Fori(0, PAIRS) as i:
                for j in range(2):
                    load_r(B - 1, i, j)
            for j in range(2):
                eng.wait_ge(psG_full[j], B * PAIRS + 1)
                eng.wait_ge(x1_st[j], B * PAIRS * 16 + 16)
            with eng.Fori(0, B) as b:
                with eng.Fori(0, PAIRS // 2) as i:
                    for j in range(4):
                        p16 = eng.snap((b * (PAIRS // 2) + i) * 16)
                        at = eng.snap((i * 4 + j) * BP)
                        eng.wait_ge(y_st[j], p16 + 16)
                        alone(eng)
                        eng.dma_start(y_buf[j][:, :, :], x1_v[bass.ds(b, 1), :, :, bass.ds(at, BP)]
                                      .rearrange("a p c n -> (a p) c n")).then_inc(y_ld[j], 16)
            for j in range(4):
                eng.wait_ge(y_st[j], B * (PAIRS // 2) * 16 + 16)
            for j in range(2):
                eng.wait_ge(v_st[j], B * PAIRS * 16 + 16)

        @block.vector
        def _(eng):
            eng.memset(taps[:, :, :], 0.0).then_inc(setup_v, 1)
            eng.memset(x1T[:, :, :, :], 1.0).then_inc(setup_v, 1)
            eng.memset(gram[:, :, :, :], 0.0).then_inc(setup_v, 1)
            eng.memset(vring[0][:, :, :, :, :], 0.0).then_inc(setup_v, 1)
            eng.memset(vring[1][:, :, :, :, :], 0.0).then_inc(setup_v, 1)
            with eng.Fori(0, B) as b:
                with eng.Fori(0, SBLK // 2) as i:
                    for j in range(2):
                        eng.wait_ge(st_ld[j], (b * (SBLK // 2) + i) * 16 + 16)
                        n = SR * W // 512
                        for c in range(CC):
                            for k in range(n):
                                at = c * SR * W + k * 512
                                ins = eng.bn_stats(
                                    bst[:, c, bass.ds((i * 2 + j) * n + k, 1), :]
                                    .rearrange("p a s -> p (a s)"),
                                    patch[j][:, :, :].rearrange("p j e -> p (j e)")[:, at:at + 512])
                        ins.then_inc(st_used[j], 1)
                for j in range(2):
                    eng.wait_ge(st_used[j], (b + 1) * (SBLK // 2) + 1)
                alone(eng)
                for c in range(CC):
                    ins = eng.bn_aggr(mv_now[:, c, :], bst[:, c, :, :].rearrange("p a s -> p (a s)"))
                ins.then_inc(st_v, 1)
                eng.wait_ge(st_v, b * 2 + 1)
                eng.tensor_copy(mv[:, :, bass.ds(b, 1), :].rearrange("p c a s -> p c (a s)"),
                                mv_now[:, :, :]).then_inc(st_v, 1)
                eng.wait_ge(st_v, b * 2 + 2)
            count = 2 * B

            def stat_step(ins):
                nonlocal count
                count += 1
                ins.then_inc(st_v, 1)
                eng.wait_ge(st_v, count)

            stat_step(eng.tensor_tensor(mean_x[:, :, :], mv[:, :, :, 0], mv[:, :, :, 0], ALU.mult))
            stat_step(eng.tensor_tensor(mv[:, :, :, 1], mv[:, :, :, 1], mean_x[:, :, :], ALU.add))
            mark["channels"] = count
            eng.wait_ge(st_p, 1)
            pg = psI[:, 0:CC * B * 2].rearrange("p (c b k) -> p c b k", b=B, k=2)
            stat_step(eng.tensor_copy(mean_x[:, :, :], pg[:, :, :, 0]))
            stat_step(eng.tensor_tensor(mv[:, :, :, 0], mean_x[:, :, :], mean_x[:, :, :], ALU.mult))
            stat_step(eng.tensor_tensor(rstd_x[:, :, :], pg[:, :, :, 1], mv[:, :, :, 0], ALU.subtract))
            stat_step(eng.tensor_scalar(rstd_x[:, :, :], rstd_x[:, :, :], 0.0, EPS_GN, ALU.max, ALU.add))
            mark["variance"] = count
            eng.wait_ge(st_a, 1)
            stat_step(eng.reciprocal(rstd_x[:, :, :], rstd_x[:, :, :]))
            eng.wait_ge(consts, 11)
            eng.wait_ge(const_ld, 16 * 7)
            eng.wait_ge(setup_v, 5)
            eng.tensor_tensor(grid[:, :, :], grid[:, :, :],
                              off_b[:, 0:2 * G].unsqueeze(1).to_broadcast([P, H, 2 * G]), ALU.add)\
               .then_inc(setup_v, 1)
            eng.tensor_scalar(first_patch[:, :, :], first_patch[:, :, :], float(W * ENT), None, ALU.mult)\
               .then_inc(setup_v, 1)
            eng.wait_ge(setup_v, 7)

            def prep(b):
                for c in range(CC):
                    eng.tensor_scalar(wB[:, c, :], wA_sb[:, c, :], rstd_x[:, c, bass.ds(b, 1)],
                                      None, ALU.mult).then_inc(w_ready, 1)
                    eng.tensor_copy(mean_bc[:, c, :],
                                    mean_x[:, c, bass.ds(b, 1)].to_broadcast([P, P]))\
                       .then_inc(w_ready, 1)
                eng.wait_ge(psI_full, b * (NQ + 1) + 1)
                eng.tensor_tensor(biasB[:, :], biasA_sb[:, :], psI[:, 0:NA], ALU.subtract)\
                   .then_inc(psI_free, 1)
                eng.wait_ge(psI_free, b * (NQ + 1) + 2)
                alone(eng)

            def conv_out(b, i, j):
                for r in range(ROWS):
                    k = r % 2
                    eng.wait_ge(row_full[j][r], b * PAIRS + i + 2)
                    if r == 0:
                        eng.wait_ge(v_st[j], (b * PAIRS + i) * 16 + 16)
                    if r == ROWS - 1:
                        eng.wait_ge(v_st[1 - j], (b * PAIRS + i + j) * 16 + 16)
                    dst = vring[j][:, r + 1, :, 0, :] if r < ROWS - 1 else vring[1 - j][:, 0, :, 0, :]
                    eng.tensor_tensor(dst, psA[k][:, 0:C].rearrange("p (g e) -> p g e", g=G),
                                      biasB[:, 0:C].rearrange("p (g e) -> p g e", g=G), ALU.add)\
                       .then_inc(v_row, 1)
                    eng.tensor_tensor(taps[:, bass.ds((i * 2 + j) * ROWS + r + 1, 1), :]
                                      .rearrange("p a n -> p (a n)"),
                                      psA[k][:, C:NA], biasB[:, C:NA], ALU.add)\
                       .then_inc(psA_free[k], 1)

            NV = 18

            def place(b):
                ix, a, bb, m0, m1 = (pt[n][:, :, :] for n in ("ix", "a", "b", "m0", "m1"))
                tm, th, w0, w1, ia = (pm[n][:, :, :] for n in ("tm", "th", "w0", "w1", "ia"))
                for q in range(NQ):
                    pq = psI[:, 0:QR * NO].rearrange("p (r o) -> p r o", o=NO)
                    base = (b * NQ + q) * NV
                    count = 0

                    def step(ins):
                        nonlocal count
                        count += 1
                        ins.then_inc(place_v, 1)
                        eng.wait_ge(place_v, base + count)

                    eng.wait_ge(psI_full, b * (NQ + 1) + 2 + q)
                    eng.tensor_tensor(tm, pq[:, :, 2 * G:NO],
                                      off_b[:, 2 * G:NO].unsqueeze(1).to_broadcast([P, QR, G]),
                                      ALU.add).then_inc(mod_in, 1)
                    eng.tensor_tensor(a, pq[:, :, 0:2 * G], grid[:, q * QR:(q + 1) * QR, :],
                                      ALU.add).then_inc(psI_free, 1)
                    eng.wait_ge(psI_free, b * (NQ + 1) + 2 + q + 1)
                    step(eng.tensor_scalar(ix, a, W / (W - 1.0), 0.5, ALU.mult, ALU.subtract))
                    step(eng.tensor_scalar(a, ix, 0.5, 0.0, ALU.subtract, ALU.max))
                    step(eng.tensor_scalar(a, a, W - 2.0, MAGIC, ALU.min, ALU.add))
                    step(eng.tensor_scalar(a, a, MAGIC, None, ALU.subtract))
                    step(eng.tensor_tensor(ix, ix, a, ALU.subtract))
                    step(eng.tensor_scalar(bb, ix, -1.0, 1.0, ALU.mult, ALU.add))
                    step(eng.scalar_tensor_tensor(m0, ix, 1.0, bb, ALU.add, ALU.min))
                    step(eng.tensor_scalar(bb, bb, 1.0, None, ALU.add))
                    step(eng.tensor_tensor(m1, ix, bb, ALU.min))
                    step(eng.scalar_tensor_tensor(ia, a[:, :, 0:G], float(ENT), first_patch[:, :, :],
                                                  ALU.mult, ALU.add))
                    step(eng.scalar_tensor_tensor(
                        index[:, q * QR * G:(q + 1) * QR * G].rearrange("p (r g) -> p r g", g=G),
                        a[:, :, G:2 * G], float(VROW), ia, ALU.mult, ALU.add))
                    eng.wait_ge(mod_out, b * NQ + q + 1)
                    step(eng.tensor_scalar(th, th, 1.0, None, ALU.add))
                    step(eng.scalar_tensor_tensor(w0, m0[:, :, G:2 * G], 0.0, th, ALU.max, ALU.mult))
                    step(eng.scalar_tensor_tensor(w1, m1[:, :, G:2 * G], 0.0, th, ALU.max, ALU.mult))
                    wv = weight[:, q * QR * G * 4:(q + 1) * QR * G * 4]\
                        .rearrange("p (r g k) -> p r g k", g=G, k=4)
                    for k, (mx, wy) in enumerate(((m0, w0), (m0, w1), (m1, w0), (m1, w1))):
                        step(eng.scalar_tensor_tensor(wv[:, :, :, k], mx[:, :, 0:G], 0.0, wy,
                                                      ALU.max, ALU.mult))
                    assert count == NV
                eng.sem_inc(placed, 1)

            def sample(b, i, j):
                for h in range(2):
                    eng.wait_ge(got[j][h], (b * PAIRS + i) * (NJ * 8) + NJ * 8)
                v4 = patch[j][:, :, :].rearrange("p t (k e) -> p (t k) e", e=CG)
                w4 = weight[:, bass.ds((i * 2 + j) * (NJ * 4), NJ * 4)].unsqueeze(2)\
                    .to_broadcast([P, NJ * 4, CG])
                eng.tensor_tensor(v4, v4, w4, ALU.mult).then_inc(weighted, 1)
                eng.wait_ge(weighted, (b * PAIRS + i) * 2 + j + 1)
                eng.tensor_tensor(patch[j][:, :, 0:ENT], patch[j][:, :, 0:ENT],
                                  patch[j][:, :, ENT:PATCH], ALU.add).then_inc(halved, 1)
                eng.wait_ge(halved, (b * PAIRS + i) * 2 + j + 1)
                eng.tensor_tensor(samp[j][:, :, :].rearrange("p r (g e) -> p (r g) e", g=G),
                                  patch[j][:, :, 0:CG], patch[j][:, :, CG:ENT], ALU.add)\
                   .then_inc(sampled[j], 1)

            def residual(b, i, j):
                eng.wait_ge(xr_ld[j], (b * PAIRS + i) * 16 + 16)
                for o in range(CC):
                    eng.wait_ge(psO_full[o], (b * PAIRS + i) * 2 + j + 2)
                    eng.scalar_tensor_tensor(xr[j][:, o, :], psO[o][:, :], bo_sb[:, o:o + 1],
                                             xr[j][:, o, :], ALU.add, ALU.add)\
                       .then_inc(psO_free[o], 1)

            def gram_add(b, i, j):
                eng.wait_ge(psG_full[j], b * PAIRS + i + 2)
                eng.wait_ge(psG_free, (b * PAIRS + i) * 2 + j + 1)
                gb = gram[:, bass.ds(b, 1), :, :].rearrange("p a c n -> p (a c n)")
                eng.tensor_tensor(gb, gb, psG[:, 0:CC * (P + 1)], ALU.add).then_inc(psG_free, 1)

            def pair(a, g, i):
                sample(g, i, 0)
                if a is not None:
                    conv_out(a, i, 0)
                residual(g, i, 0)
                sample(g, i, 1)
                if a is not None:
                    conv_out(a, i, 1)
                gram_add(g, i, 0)
                residual(g, i, 1)
                gram_add(g, i, 1)

            prep(0)
            with eng.Fori(0, PAIRS) as i:
                for j in range(2):
                    conv_out(0, i, j)
            place(0)
            with eng.Fori(0, B - 1) as b:
                prep(b + 1)
                with eng.Fori(0, PAIRS) as i:
                    pair(b + 1, b, i)
                place(b + 1)
            with eng.Fori(0, PAIRS) as i:
                pair(None, B - 1, i)

            done = 0

            def step(ins):
                nonlocal done
                done += 1
                ins.then_inc(wh_v, 1)
                eng.wait_ge(wh_v, done)

            eng.wait_ge(psG_free, B * BLOCKS + 1)
            step(eng.tensor_copy(sums, gram[:, :, :, P:P + 1].rearrange("p b c n -> p c (b n)")))
            step(eng.tensor_scalar(st2[:, :, :, 0], sums, 1.0 / PIX, None, ALU.mult))
            for c in range(CC):
                step(eng.tensor_tensor(scr[:, c, :, :], gram[:, :, c, 0:P],
                                       ident[:, :].unsqueeze(1).to_broadcast([P, B, P]), ALU.mult))
            step(eng.tensor_reduce(var, scr, AX_X, ALU.add))
            step(eng.tensor_scalar(st2[:, :, :, 1], var, 1.0 / PIX, None, ALU.mult))
            mark["w_channels"] = done
            eng.wait_ge(wh_p, P_STATS)
            step(eng.tensor_copy(gm, pg[:, :, :, 0]))
            step(eng.tensor_tensor(var, gm, gm, ALU.mult))
            step(eng.tensor_tensor(var, pg[:, :, :, 1], var, ALU.subtract))
            step(eng.tensor_scalar(var, var, 0.0, EPS_GN, ALU.max, ALU.add))
            mark["w_variance"] = done
            eng.wait_ge(wh_a, 1)
            step(eng.reciprocal(rs, var))
            step(eng.tensor_tensor(g_b, gm, rs, ALU.mult))
            step(eng.tensor_tensor(a_b, sums, rs, ALU.mult))
            step(eng.scalar_tensor_tensor(d_b, g_b, float(PIX), a_b, ALU.mult, ALU.subtract))
            step(eng.tensor_reduce(mu, d_b, AX_X, ALU.add))
            step(eng.tensor_scalar(mu, mu, -1.0 / (B * PIX), None, ALU.mult))
            for c in range(CC):
                for b in range(B):
                    step(eng.tensor_scalar(scr[:, c, b, :], gram[:, b, c, 0:P], rs[:, c, b:b + 1],
                                           None, ALU.mult))
            mark["w_scaled"] = done
            for c in range(CC):
                eng.wait_ge(wh_p, P_ROWS + c)
                step(eng.tensor_copy(rowsT[0:B, c, 0, :], psT[c][0:B, 0:P]))
                step(eng.tensor_scalar(rowsT[0:B, c, 1, :], psT[c][0:B, P:2 * P], -1.0, None, ALU.mult))
                step(eng.tensor_copy(rowsT[0:B, c, 2, :], psT[c][0:B, 2 * P:3 * P]))
                step(eng.tensor_copy(rowsT[0:1, c, 3, :], psT[c][0:1, 3 * P:4 * P]))
                step(eng.tensor_scalar(T[0:1, c, :], rowsT[0:1, c, 3, :], -float(B * PIX), None,
                                       ALU.mult))
            mark["w_rows"] = done
            for c in range(CC):
                for b in range(B):
                    n = c * B + b
                    eng.wait_ge(wh_p, P_GRAM + n)
                    if b == 0:
                        step(eng.tensor_scalar(cov[:, c, :], psA[n % 2][:, 0:P], rs[:, c, b:b + 1],
                                               None, ALU.mult))
                    else:
                        step(eng.scalar_tensor_tensor(cov[:, c, :], psA[n % 2][:, 0:P],
                                                      rs[:, c, b:b + 1], cov[:, c, :],
                                                      ALU.mult, ALU.add))
            for c in range(CC):
                eng.wait_ge(wh_p, P_CROSS + c)
                step(eng.tensor_tensor(cov[:, c, :], cov[:, c, :], psO[c][:, 0:P], ALU.add))
                step(eng.scalar_tensor_tensor(cov[:, c, :], cov[:, c, :], 1.0 / (B * PIX),
                                              same16[:, :], ALU.mult, ALU.mult))
                step(eng.scalar_tensor_tensor(cov[:, c, :], ident[:, :], EPS_Z, cov[:, c, :],
                                              ALU.mult, ALU.add))
                step(eng.tensor_tensor(Y[:, c, :], cov[:, c, :], ident[:, :], ALU.mult))
            step(eng.tensor_reduce(tr, Y, AX_X, ALU.add))
            mark["w_trace"] = done
            eng.wait_ge(wh_p, P_TRACE)
            step(eng.tensor_copy(tr, psI[:, 0:CC]))
            mark["w_root"] = done
            step(eng.reciprocal(rtr, tr))
            for c in range(CC):
                step(eng.tensor_scalar(Y[:, c, :], cov[:, c, :], rtr[:, c:c + 1], None, ALU.mult))
                step(eng.tensor_copy(Z[:, c, :], ident[:, :]))
            step(eng.tensor_scalar(i15, ident[:, :], 1.5, None, ALU.mult))
            eng.sem_inc(ns_new, 1)
            with eng.Fori(0, STEPS) as s:
                for c in range(CC):
                    eng.wait_ge(ns_zy, s * CC + c + 1)
                    eng.scalar_tensor_tensor(T[:, c, :], psA[c][:, 0:P], -0.5, i15, ALU.mult,
                                             ALU.add).then_inc(ns_t, 1)
                for c in range(CC):
                    eng.wait_ge(ns_zt, s * CC + c + 1)
                    eng.tensor_copy(Y[:, c, :], psT[c][:, 0:P])
                    ins = eng.tensor_copy(Z[:, c, :], psO[c][:, 0:P])
                ins.then_inc(ns_new, 1)
            eng.wait_ge(ns_new, STEPS + 1)
            eng.wait_ge(wh_a, 2)
            step(eng.reciprocal(srt, srt))
            for c in range(CC):
                step(eng.tensor_scalar(dg[:, c, :], ident[:, :], wz_sb[:, c:c + 1], None, ALU.mult))
            mark["w_root_of_cov"] = done
            for c in range(CC):
                eng.wait_ge(wh_p, P_PW + c)
                step(eng.tensor_scalar(pw[:, c, :], psA[c][:, 0:P], srt[:, c:c + 1], None, ALU.mult))
                step(eng.tensor_scalar(gmu[:, c, :], g_b[:, c, :], mu[:, c:c + 1], None, ALU.add))
            mark["w_pw"] = done
            for c in range(CC):
                eng.wait_ge(wh_p, P_CST + CC - 1)
                step(eng.tensor_scalar(cst[:, c, :], psG[:, c * B:(c + 1) * B], -1.0,
                                       bz_sb[:, c:c + 1], ALU.mult, ALU.add))
            with eng.Fori(0, B) as b:
                for j in range(4):
                    eng.wait_ge(y_add[j], b * (PAIRS // 2) + 1)
                for c in range(CC):
                    eng.tensor_scalar(amap[:, c, :], pw[:, c, :], rs[:, c, bass.ds(b, 1)], None,
                                      ALU.mult).then_inc(map_v, 1)
                    eng.tensor_copy(cnow[:, c:c + 1], cst[:, c, bass.ds(b, 1)]).then_inc(map_v, 1)
                eng.wait_ge(map_v, (b + 1) * (2 * CC))
                alone(eng)
                with eng.Fori(0, PAIRS // 2) as i:
                    for j in range(4):
                        eng.wait_ge(y_mm[j], b * (PAIRS // 2) + i + 1)
                        for c in range(CC):
                            ins = eng.scalar_tensor_tensor(y_buf[j][:, c, :], y_bank[j][c][:, :],
                                                           cnow[:, c:c + 1], y_buf[j][:, c, :],
                                                           ALU.add, ALU.add)
                        ins.then_inc(y_add[j], 1)

        @block.gpsimd
        def _(eng):
            for free in (*st_used, *row_full[0], *row_full[1], *sampled, *psT_free, *psO_free,
                         *psO_full, *psG_full, psG_free, *psA_free, psI_free, *y_add):
                eng.sem_inc(free, 1)
            eng.memset(ident[:, :], 0.0).then_inc(zeros, 1)
            eng.memset(shift[:, :, :], 0.0).then_inc(zeros, 1)
            eng.memset(avg8[:, :], 1.0 / GN1).then_inc(zeros, 1)
            eng.memset(same16[:, :], 1.0).then_inc(zeros, 1)
            eng.wait_ge(zeros, 4)
            eng.affine_select(out=ident[:, :], in_=ident[:, :], compare_op=ALU.not_equal, fill=1.0,
                              base=0, pattern=[[-1, P]], channel_multiplier=1).then_inc(consts, 1)
            for d in range(3):
                eng.affine_select(out=shift[:, d, :], in_=shift[:, d, :], compare_op=ALU.not_equal,
                                  fill=1.0, base=1 - d, pattern=[[-1, P]],
                                  channel_multiplier=1).then_inc(consts, 1)
            done = 4
            for m, g in ((avg8, GN1), (same16, GZ)):
                eng.affine_select(out=m[:, :], in_=m[:, :], compare_op=ALU.is_ge, fill=0.0, base=0,
                                  pattern=[[-g, P // g], [0, g]],
                                  channel_multiplier=1).then_inc(consts, 1)
                done += 1
                eng.wait_ge(consts, done)
                eng.affine_select(out=m[:, :], in_=m[:, :], compare_op=ALU.is_ge, fill=0.0,
                                  base=g - 1, pattern=[[g, P // g], [0, g]],
                                  channel_multiplier=-1).then_inc(consts, 1)
                done += 1
            eng.iota(grid[:, :, 0:G], pattern=[[0, H], [0, G]], base=0, channel_multiplier=1,
                     allow_small_or_imprecise_dtypes=True).then_inc(consts, 1)
            eng.iota(grid[:, :, G:2 * G], pattern=[[1, H], [0, G]], base=0, channel_multiplier=0,
                     allow_small_or_imprecise_dtypes=True).then_inc(consts, 1)
            eng.iota(first_patch[:, :, :], pattern=[[0, QR], [1, G]], base=G, channel_multiplier=0,
                     allow_small_or_imprecise_dtypes=True).then_inc(consts, 1)

            def gather(b, k, i, j):
                eng.wait_ge(sampled[j], b * PAIRS + i + 1)
                eng.tensor_copy(index_now[j][:, :],
                                index[:, bass.ds((i * 2 + j) * NJ, NJ)]).then_inc(index_cp, 1)
                eng.wait_ge(index_cp, (b * PAIRS + i) * 2 + j + 1)
                alone(eng)
                for t in range(NJ):
                    eng.indirect_dma_start(
                        out=patch[j][:, t, :], out_offset=None, in_=v2_flat[k],
                        in_offset=bass.IndirectOffsetOnAxis(ap=index_now[j][:, t:t + 1], axis=1),
                    ).then_inc(got[j][t // (NJ // 2)], 16)

            def gather_image(b, k):
                eng.wait_ge(placed, b + 1)
                for j in range(2):
                    eng.wait_ge(v_st[j], (b + 1) * (PAIRS * 16) + 16)
                alone(eng)
                with eng.Fori(0, PAIRS) as i:
                    for j in range(2):
                        gather(b, k, i, j)

            images(eng, 0, B, gather_image)

        def whiten_tensor(eng):
            eng.wait_ge(wh_v, mark["w_channels"])
            eng.matmul(psI[:, 0:CC * B * 2], avg8[:, :],
                       st2.rearrange("p c b k -> p (c b k)"), start=True, stop=True)\
               .then_inc(wh_p, 1)
            eng.wait_ge(wh_v, mark["w_scaled"])
            for c in range(CC):
                for k, m in enumerate((g_b, a_b, d_b)):
                    eng.matmul(psT[c][0:B, k * P:(k + 1) * P], m[:, c, :], ident[:, :],
                               start=True, stop=True)
                eng.matmul(psT[c][0:1, 3 * P:4 * P], mu[:, c:c + 1], ident[:, :],
                           start=True, stop=True).then_inc(wh_p, 1)
            for c in range(CC):
                for b in range(B):
                    n = c * B + b
                    if n >= 2:
                        eng.wait_ge(wh_v, mark["w_rows"] + n - 1)
                    eng.matmul(psA[n % 2][:, 0:P], scr[:, c, b, :], ident[:, :],
                               start=True, stop=True).then_inc(wh_p, 1)
            eng.wait_ge(wh_v, mark["w_rows"])
            for c in range(CC):
                eng.matmul(psO[c][:, 0:P], rowsT[0:B, c, 1, :], rowsT[0:B, c, 0, :],
                           start=True, stop=False)
                eng.matmul(psO[c][:, 0:P], rowsT[0:B, c, 0, :], rowsT[0:B, c, 2, :],
                           start=False, stop=False)
                eng.matmul(psO[c][:, 0:P], rowsT[0:1, c, 3, :], T[0:1, c, :],
                           start=False, stop=True).then_inc(wh_p, 1)
            eng.wait_ge(wh_v, mark["w_trace"])
            eng.matmul(psI[:, 0:CC], same16[:, :], tr, start=True, stop=True).then_inc(wh_p, 1)
            with eng.Fori(0, STEPS) as s:
                eng.wait_ge(ns_new, s + 1)
                for c in range(CC):
                    eng.matmul(psA[c][:, 0:P], Z[:, c, :], Y[:, c, :], start=True, stop=True)\
                       .then_inc(ns_zy, 1)
                for c in range(CC):
                    eng.wait_ge(ns_t, s * CC + c + 1)
                    eng.matmul(psT[c][:, 0:P], Y[:, c, :], T[:, c, :], start=True, stop=True)
                    eng.matmul(psO[c][:, 0:P], T[:, c, :], Z[:, c, :], start=True, stop=True)\
                       .then_inc(ns_zt, 1)
            eng.wait_ge(wh_v, mark["w_root_of_cov"])
            for c in range(CC):
                eng.matmul(psA[c][:, 0:P], Z[:, c, :], dg[:, c, :], start=True, stop=True)\
                   .then_inc(wh_p, 1)
            eng.wait_ge(wh_v, mark["w_pw"])
            for c in range(CC):
                eng.matmul(psG[:, c * B:(c + 1) * B], pw[:, c, :], gmu[:, c, :],
                           start=True, stop=True).then_inc(wh_p, 1)

        @block.tensor
        def _(eng):
            eng.wait_ge(consts, 11)
            eng.wait_ge(const_ld, 16 * 7)
            eng.wait_ge(st_v, mark["channels"])
            eng.matmul(psI[:, 0:CC * B * 2], avg8[:, :],
                       mv[:, :, :, :].rearrange("p c b k -> p (c b k)"),
                       start=True, stop=True).then_inc(st_p, 1)

            def prep(b):
                eng.wait_ge(w_ready, (b + 1) * 4)
                eng.wait_ge(psI_free, b * (NQ + 1) + 1)
                for c in range(CC):
                    mm = eng.matmul(psI[:, 0:NA], mean_bc[:, c, :], wB[:, c, :],
                                    start=(c == 0), stop=(c == CC - 1))
                mm.then_inc(psI_full, 1)

            def conv_rows(b, i, j, rows):
                if 0 in rows:
                    eng.wait_ge(xa_ld[j], (b * PAIRS + i) * 16 + 16)
                for r in rows:
                    k = r % 2
                    eng.wait_ge(psA_free[k], (b * PAIRS + i) * 4 + 2 * j + r // 2 + 1)
                    for c in range(CC):
                        mm = eng.matmul(psA[k][:, 0:NA], xa[j][:, c, r * W:(r + 1) * W],
                                        wB[:, c, :], start=(c == 0), stop=(c == CC - 1))
                    mm.then_inc(row_full[j][r], 1)

            def offsets(b):
                for k in range(2):
                    eng.wait_ge(psA_free[k], (b + 1) * (PAIRS * 4) + 1)
                for q in range(NQ):
                    eng.wait_ge(psI_free, b * (NQ + 1) + 1 + q + 1)
                    for t in range(NTAP):
                        dy, dx = t // 3, t % 3
                        mm = eng.matmul(psI[:, 0:QR * NO].rearrange("p (r o) -> p r o", o=NO),
                                        shift[:, dx, :],
                                        taps[:, q * QR + dy:q * QR + dy + QR, t * NO:(t + 1) * NO],
                                        start=(t == 0), stop=(t == NTAP - 1))
                    mm.then_inc(psI_full, 1)

            def turn_samples(b, i, j):
                eng.wait_ge(sampled[j], b * PAIRS + i + 2)
                for h in range(CC):
                    eng.wait_ge(psT_free[h], (b * PAIRS + i) * 4 + 2 * j + 1)
                    for r in range(ROWS):
                        mm = eng.transpose(psT[h][:, r * W:(r + 1) * W],
                                           samp[j][:, r, h * P:(h + 1) * P], ident[:, :])
                    mm.then_inc(psT_full[h], 1)

            def out_conv(b, i, j):
                for h in range(CC):
                    eng.wait_ge(psT_free[h], (b * PAIRS + i) * 4 + 2 * j + 2)
                for o in range(CC):
                    eng.wait_ge(psO_free[o], (b * PAIRS + i) * 2 + j + 1)
                    for h in range(CC):
                        mm = eng.matmul(psO[o][:, :], wO_sb[:, h, o * P:(o + 1) * P],
                                        sampT[:, h, :], start=(h == 0), stop=(h == CC - 1))
                    mm.then_inc(psO_full[o], 1)

            def turn_x1(b, i, j):
                for o in range(CC):
                    eng.wait_ge(psO_free[o], (b * PAIRS + i) * 2 + j + 2)
                for h in range(2):
                    eng.wait_ge(psT_free[h], (b * PAIRS + i) * 4 + 2 * j + 2)
                    for r in range(2):
                        for c in range(CC):
                            at = (r * CC + c) * P
                            row = 2 * h + r
                            mm = eng.transpose(psT[h][:, at:at + P],
                                               xr[j][:, c, row * W:(row + 1) * W], ident[:, :])
                    mm.then_inc(psT_full[h], 1)

            def gram_block(b, i, j):
                for h in range(2):
                    eng.wait_ge(psT_free[h], (b * PAIRS + i) * 4 + 2 * j + 3)
                eng.wait_ge(psG_free, (b * PAIRS + i) * 2 + j + 1)
                for c in range(CC):
                    for r in range(ROWS):
                        mm = eng.matmul(psG[:, c * (P + 1):(c + 1) * (P + 1)], x1T[:, r, c, 0:P],
                                        x1T[:, r, c, :], start=(r == 0), stop=(r == ROWS - 1))
                mm.then_inc(psG_full[j], 1)

            def pair(a, g, i):
                def conv(j, rows):
                    if a is not None:
                        conv_rows(a, i, j, rows)
                conv(0, (0, 1))
                turn_samples(g, i, 0)
                conv(0, (2, 3))
                out_conv(g, i, 0)
                conv(1, (0, 1))
                turn_x1(g, i, 0)
                turn_samples(g, i, 1)
                gram_block(g, i, 0)
                conv(1, (2, 3))
                out_conv(g, i, 1)
                turn_x1(g, i, 1)
                gram_block(g, i, 1)

            prep(0)
            with eng.Fori(0, PAIRS) as i:
                for j in range(2):
                    conv_rows(0, i, j, range(ROWS))
            offsets(0)
            with eng.Fori(0, B - 1) as b:
                prep(b + 1)
                with eng.Fori(0, PAIRS) as i:
                    pair(b + 1, b, i)
                offsets(b + 1)
            with eng.Fori(0, PAIRS) as i:
                pair(None, B - 1, i)
            whiten_tensor(eng)
            with eng.Fori(0, B) as b:
                eng.wait_ge(map_v, (b + 1) * (2 * CC))
                alone(eng)
                with eng.Fori(0, PAIRS // 2) as i:
                    for j in range(4):
                        eng.wait_ge(y_ld[j], (b * (PAIRS // 2) + i) * 16 + 16)
                        eng.wait_ge(y_add[j], b * (PAIRS // 2) + i + 1)
                        for c in range(CC):
                            mm = eng.matmul(y_bank[j][c][:, :], amap[:, c, :], y_buf[j][:, c, :],
                                            start=True, stop=True)
                        mm.then_inc(y_mm[j], 1)

        @block.scalar
        def _(eng):
            eng.wait_ge(st_v, mark["variance"])
            eng.activation(rstd_x[:, :, :], rstd_x[:, :, :], ACT.Sqrt).then_inc(st_a, 1)

            def dup(b, k, i, j):
                for r in range(ROWS):
                    src = vring[j][:, r + 1, :, 0, :] if r < ROWS - 1 else vring[1 - j][:, 0, :, 0, :]
                    eng.wait_ge(v_row, (b * PAIRS + i) * 8 + 4 * j + r + 1)
                    eng.activation(vring[j][:, r, :, 1, :], src, ACT.Copy).then_inc(v_dup, 1)
                row = eng.snap((i * 2 + j) * NJ)
                eng.wait_ge(v_dup, (b * PAIRS + i) * 8 + 4 * j + 4)
                eng.dma_start(v2_rows[k][:, bass.ds(row, NJ), :],
                              vring[j][:, :, :, :, :].rearrange("p r g k e -> p (r g) (k e)"))\
                   .then_inc(v_st[j], 16)

            def samples_out(b, i, j):
                eng.wait_ge(psO_full[CC - 1], (b * PAIRS + i) * 2 + j + 1)
                for h in range(CC):
                    eng.wait_ge(psT_full[h], (b * PAIRS + i) * 4 + 2 * j + 1)
                    eng.activation(sampT[:, h, :], psT[h][:, :], ACT.Copy).then_inc(psT_free[h], 1)

            def x1_store(b, i, j):
                at = eng.snap((i * 2 + j) * BP)
                bb = eng.snap(b) if not isinstance(b, int) else b
                for o in range(CC):
                    eng.wait_ge(psO_free[o], (b * PAIRS + i) * 2 + j + 2)
                eng.dma_start(x1_v[bass.ds(bb, 1), :, :, bass.ds(at, BP)]
                              .rearrange("a p c n -> (a p) c n"), xr[j][:, :, :])\
                   .then_inc(x1_st[j], 16)

            def x1_out(b, i, j):
                eng.wait_ge(psG_full[1 - j], b * PAIRS + i + j + 1)
                for h in range(2):
                    eng.wait_ge(psT_full[h], (b * PAIRS + i) * 4 + 2 * j + 2)
                    eng.activation(x1T[:, 2 * h:2 * h + 2, :, 0:P].rearrange("p r c n -> p (r c) n"),
                                   psT[h][:, :].rearrange("p (q n) -> p q n", n=P), ACT.Copy)\
                       .then_inc(psT_free[h], 1)

            def modulation(b):
                for q in range(NQ):
                    eng.wait_ge(mod_in, b * NQ + q + 1)
                    eng.activation(pm["th"][:, :, :], pm["tm"][:, :, :], ACT.Tanh).then_inc(mod_out, 1)

            def conv_image(b, k):
                with eng.Fori(0, PAIRS) as i:
                    for j in range(2):
                        samples_out(b - 1, i, j)
                        dup(b, k, i, j)
                        x1_store(b - 1, i, j)
                        x1_out(b - 1, i, j)
                modulation(b)

            with eng.Fori(0, PAIRS) as i:
                for j in range(2):
                    dup(0, 0, i, j)
            modulation(0)
            images(eng, 1, B, conv_image)
            with eng.Fori(0, PAIRS) as i:
                for j in range(2):
                    samples_out(B - 1, i, j)
                    x1_store(B - 1, i, j)
                    x1_out(B - 1, i, j)
            eng.wait_ge(wh_v, mark["w_variance"])
            eng.activation(var, var, ACT.Sqrt).then_inc(wh_a, 1)
            eng.wait_ge(wh_v, mark["w_root"])
            eng.activation(srt, tr, ACT.Sqrt).then_inc(wh_a, 1)
            with eng.Fori(0, B) as b:
                with eng.Fori(0, PAIRS // 2) as i:
                    for j in range(4):
                        at = eng.snap((i * 4 + j) * BP)
                        eng.wait_ge(y_add[j], b * (PAIRS // 2) + i + 2)
                        eng.dma_start(out_v[bass.ds(b, 1), :, :, bass.ds(at, BP)]
                                      .rearrange("a p c n -> (a p) c n"), y_buf[j][:, :, :])\
                           .then_inc(y_st[j], 16)


def kernel(x, L0_conv_offset_w, L0_conv_offset_b, L0_conv_mod_w, L0_conv_mod_b, L0_conv_kv_w,
           L0_conv_kv_b, L0_conv_out_w, L0_conv_out_b, L1_conv_weight, L1_conv_bias):
    import numpy as np
    import concourse.bacc as bacc
    from concourse.bass_utils import run_bass_kernel_spmd

    arr = lambda a: np.ascontiguousarray(a)
    B = x.shape[0]
    heads = C // 32
    perm = np.arange(C).reshape(heads // G, G, 32).transpose(1, 0, 2).reshape(-1)
    order = np.arange(2 * G).reshape(G, 2).T.reshape(-1)
    kv_w = np.asarray(L0_conv_kv_w)[C:, :, 0, 0][perm]
    kv_b = np.asarray(L0_conv_kv_b)[C:][perm]
    taps = np.concatenate([np.asarray(L0_conv_offset_w)[order], np.asarray(L0_conv_mod_w)])
    off_b = np.concatenate([np.asarray(L0_conv_offset_b)[order], np.asarray(L0_conv_mod_b)])
    arrays = {
        "x_dram": arr(x),
        "wA_dram": arr(np.concatenate([kv_w.T, taps.transpose(1, 2, 3, 0).reshape(C, NT)], 1)),
        "biasA_dram": arr(np.concatenate([kv_b, np.zeros(NT, kv_b.dtype)])),
        "bias_off_dram": arr(off_b),
        "wO_dram": arr(np.asarray(L0_conv_out_w)[:, :, 0, 0].T[perm]),
        "bias_o_dram": arr(np.asarray(L0_conv_out_b).reshape(CC, P).T),
        "w_z_dram": arr(np.asarray(L1_conv_weight).reshape(CC, P).T),
        "bias_z_dram": arr(np.asarray(L1_conv_bias).reshape(CC, P).T),
    }
    nc = bacc.Bacc("TRN2", target_bir_lowering=False, num_devices=1)
    args = [nc.dram_tensor(n, a.shape, mybir.dt.from_np(a.dtype), kind="ExternalInput").ap()
            for n, a in arrays.items()]
    out = nc.dram_tensor("out_dram", x.shape, F32, kind="ExternalOutput").ap()
    deform_zca_kernel(nc, B, *args, out)
    r = run_bass_kernel_spmd(nc, [arrays], core_ids=[0])
    return r.results[0]["out_dram"]
```

```python
from contextlib import ExitStack

import concourse.bass as bass
from concourse import mybir

ALU = mybir.AluOpType
ACT = mybir.ActivationFunctionType
AX_X = mybir.AxisListType.X
F32 = mybir.dt.float32
U32 = mybir.dt.uint32

P = 128
C, H, W = 256, 128, 128
PIX = H * W
CC = C // P
G = 4
CG = C // G
NTAP = 9
NO = 3 * G
NT = NTAP * NO
NA = C + NT
ROWS = 4
BP = ROWS * W
BLOCKS = H // ROWS
PAIRS = BLOCKS // 2
NJ = ROWS * G
PATCH = 4 * CG
ENT = 2 * CG
VROWS = H
VROW = G * W * ENT
IMG = VROWS * VROW
QR = 2 * ROWS
NQ = H // QR
NH = NJ // 2
YB = 2 * BP
NY = 4
GN1 = 8
GZ = 16
EPS_GN, EPS_Z = 1e-5, 1e-4
MAGIC = 12582912.0
STEPS = 24


def deform_zca_kernel(nc, B, x, wA, biasA, bias_off, wO, bias_o, w_z, bias_z, out):
    v2 = [nc.dram_tensor(f"v2_{j}", [IMG], F32, kind="Internal").ap() for j in range(2)]
    x1 = nc.dram_tensor("x1", [B, CC, P, PIX], F32, kind="Internal").ap()
    x_v = x.rearrange("b (c p) h w -> b p c (h w)", p=P)
    out_v = out.rearrange("b (c p) h w -> b p c (h w)", p=P)
    x1_v = x1.rearrange("b c p n -> b p c n")
    v2_flat = [v.rearrange("(a n) -> a n", a=1) for v in v2]
    v2_rows = [v.rearrange("(r x e) -> x r e", x=W, e=ENT) for v in v2]

    ctx = ExitStack()
    with ctx:
        def sb(name, shape, dt=F32):
            return ctx.enter_context(nc.sbuf_tensor(name, shape, dt))

        def ps(name):
            return ctx.enter_context(nc.psum_tensor(name, [P, 512], F32))

        def sem(name):
            return ctx.enter_context(nc.semaphore(name))

        ident = sb("ident", [P, P])
        shift = sb("shift", [P, 3, P])
        avg8 = sb("avg8", [P, P])
        same16 = sb("same16", [P, P])
        wA_sb = sb("wA_sb", [P, CC, NA])
        wO_sb = sb("wO_sb", [P, CC, C])
        biasA_sb = sb("biasA_sb", [P, NA])
        off_b = sb("off_b", [P, NO])
        bo_sb = sb("bo_sb", [P, CC])
        wz_sb = sb("wz_sb", [P, CC])
        bz_sb = sb("bz_sb", [P, CC])
        grid = sb("grid", [P, H, 2 * G])
        first_patch = sb("first_patch", [P, QR, G])
        opening = sb("opening", [P, 8, CC])
        wB = sb("wB", [P, CC, NA])
        mean_bc = sb("mean_bc", [P, CC, P])
        biasB = sb("biasB", [P, NA])
        taps = sb("taps", [P, H + 2, NT])
        index = sb("index", [P, H * G], U32)
        weight = sb("weight", [P, H * G * 4])
        xa = [sb(f"xa{j}", [P, CC, BP]) for j in range(2)]
        vring = [sb(f"vring{j}", [P, ROWS, G, 2, CG]) for j in range(2)]
        carry = [sb(f"carry{j}", [P, G, CG]) for j in range(2)]
        index_now = [sb(f"index_now{j}", [P, NJ], U32) for j in range(2)]
        patch = [sb(f"patch{j}", [P, NJ, PATCH]) for j in range(2)]
        samp = [sb(f"samp{j}", [P, ROWS, C]) for j in range(2)]
        sampT = sb("sampT", [P, CC, BP])
        xr = [sb(f"xr{j}", [P, CC, BP]) for j in range(2)]
        x1T = sb("x1T", [P, ROWS, CC, P + 1])
        gram = sb("gram", [P, B, CC, P + 1])
        xs = [sb(f"xs{j}", [P, CC, BP]) for j in range(2)]
        bst = sb("bst", [P, CC, BLOCKS, 6])
        mv = sb("mv", [P, CC, 2])
        msq = sb("msq", [P, CC])
        mean_x = sb("mean_x", [P, CC])
        rstd_x = sb("rstd_x", [P, CC])
        pt = {n: sb("p_" + n, [P, QR, 2 * G]) for n in ("ix", "a", "b", "m0", "m1")}
        pm = {n: sb("p_" + n, [P, QR, G]) for n in ("tm", "th", "w0", "w1", "ia")}

        psA = [ps(f"psA{i}") for i in range(2)]
        psI = ps("psI")
        psT = [ps(f"psT{i}") for i in range(2)]
        psO = [ps(f"psO{i}") for i in range(2)]
        psG = ps("psG")

        NU = 2 + NQ
        const_ld = sem("const_ld")
        consts = sem("consts")
        zeros = sem("zeros")
        passed = sem("passed")
        setup_v = sem("setup_v")
        st_ld = [sem(f"st_ld{j}") for j in range(2)]
        st_used = [sem(f"st_used{j}") for j in range(2)]
        st_v = sem("st_v")
        st_a = sem("st_a")
        xa_ld = [sem(f"xa_ld{j}") for j in range(2)]
        row_full = [[sem(f"row_full{j}{r}") for r in range(ROWS)] for j in range(2)]
        psA_free = [sem(f"psA_free{j}") for j in range(2)]
        v_row = sem("v_row")
        v_dup = sem("v_dup")
        v_st = [sem(f"v_st{j}") for j in range(2)]
        w_ready = sem("w_ready")
        psI_full = sem("psI_full")
        psI_free = sem("psI_free")
        place_v = sem("place_v")
        mod_in = sem("mod_in")
        mod_out = sem("mod_out")
        placed = sem("placed")
        index_cp = sem("index_cp")
        got = [[sem(f"got{j}{h}") for h in range(2)] for j in range(2)]
        weighted = sem("weighted")
        halved = sem("halved")
        sampled = [[sem(f"sampled{j}{h}") for h in range(2)] for j in range(2)]
        psT_full = [sem(f"psT_full{j}") for j in range(2)]
        psT_free = [sem(f"psT_free{j}") for j in range(2)]
        psO_full = [sem(f"psO_full{j}") for j in range(2)]
        psO_free = [sem(f"psO_free{j}") for j in range(2)]
        xr_ld = [sem(f"xr_ld{j}") for j in range(2)]
        x1_st = [sem(f"x1_st{j}") for j in range(2)]
        psG_full = [sem(f"psG_full{j}") for j in range(2)]
        psG_free = sem("psG_free")
        wh_v = sem("wh_v")
        wh_p = sem("wh_p")
        wh_a = sem("wh_a")
        ns_t = sem("ns_t")
        ns_zy = sem("ns_zy")
        ns_zt = sem("ns_zt")
        ns_new = sem("ns_new")
        map_v = sem("map_v")
        y_ld = [sem(f"y_ld{j}") for j in range(NY)]
        y_mm = [sem(f"y_mm{j}") for j in range(NY)]
        y_add = [sem(f"y_add{j}") for j in range(NY)]
        y_st = [sem(f"y_st{j}") for j in range(NY)]

        wk = patch[0][:, :, :].rearrange("p j e -> p (j e)")
        wk2 = patch[1][:, :, :].rearrange("p j e -> p (j e)")

        def area(base, at, n):
            return base[:, at:at + n]

        def alone(eng):
            eng.sem_inc(passed, 1)

        def run(eng, image):
            image(None, None, 0)
            image(None, 0, 1)
            if B > 2:
                with eng.Fori(0, B - 2) as b:
                    image(b, b + 1, b + 2)
            image(B - 2, B - 1, None)
            image(B - 1, None, None)

        def pairs(eng, pair):
            pair(0)
            with eng.Fori(1, PAIRS - 1) as i:
                pair(i)
            pair(PAIRS - 1)

        block = ctx.enter_context(nc.Block())

        gm = area(wk, 0, CC * B).rearrange("p (c b) -> p c b", b=B)
        rs = area(wk, 16, CC * B).rearrange("p (c b) -> p c b", b=B)
        sums = area(wk, 32, CC * B).rearrange("p (c b) -> p c b", b=B)
        st2 = area(wk, 48, CC * B * 2).rearrange("p (c b k) -> p c b k", b=B, k=2)
        g_b = area(wk, 80, CC * B).rearrange("p (c b) -> p c b", b=B)
        a_b = area(wk, 96, CC * B).rearrange("p (c b) -> p c b", b=B)
        d_b = area(wk, 112, CC * B).rearrange("p (c b) -> p c b", b=B)
        mu = area(wk, 128, CC)
        gmu = area(wk, 136, CC * B).rearrange("p (c b) -> p c b", b=B)
        cst = area(wk, 152, CC * B).rearrange("p (c b) -> p c b", b=B)
        tr = area(wk, 168, CC)
        rtr = area(wk, 172, CC)
        srt = area(wk, 176, CC)
        var = area(wk, 184, CC * B).rearrange("p (c b) -> p c b", b=B)
        scr = area(wk, 256, CC * B * P).rearrange("p (c b n) -> p c b n", b=B, n=P)
        cov = area(wk2, 0, CC * P).rearrange("p (c n) -> p c n", n=P)
        Y = area(wk2, 256, CC * P).rearrange("p (c n) -> p c n", n=P)
        Z = area(wk2, 512, CC * P).rearrange("p (c n) -> p c n", n=P)
        T = area(wk2, 768, CC * P).rearrange("p (c n) -> p c n", n=P)
        rowsT = area(wk2, 1024, CC * 4 * P).rearrange("p (c k n) -> p c k n", k=4, n=P)
        dg = area(wk2, 2048, CC * P).rearrange("p (c n) -> p c n", n=P)
        pw = area(wk2, 2304, CC * P).rearrange("p (c n) -> p c n", n=P)
        amap = area(wk2, 2560, CC * P).rearrange("p (c n) -> p c n", n=P)
        i15 = area(wk2, 2816, P)
        cnow = area(wk2, 2944, CC)
        y_mem = taps[:, :, :].rearrange("p r n -> p (r n)")
        y_buf = [area(y_mem, n * CC * YB, CC * YB).rearrange("p (c n) -> p c n", c=CC)
                 for n in range(NY)]
        y_bank = ((*psO, *psA), (*psT, psI, psG))
        mark = {}


        P_STATS = 1
        P_ROWS = P_STATS + 1
        P_GRAM = P_ROWS + CC
        P_CROSS = P_GRAM + CC * B
        P_TRACE = P_CROSS + CC
        P_PW = P_TRACE + 1
        P_CST = P_PW + CC

        @block.sync
        def _(eng):
            for dst, src in ((wA_sb[:, :, :], wA.rearrange("(c p) n -> p c n", p=P)),
                             (wO_sb[:, :, :], wO.rearrange("(c p) n -> p c n", p=P)),
                             (biasA_sb[:, :], biasA.partition_broadcast(P)),
                             (off_b[:, :], bias_off.partition_broadcast(P)),
                             (bo_sb[:, :], bias_o), (wz_sb[:, :], w_z), (bz_sb[:, :], bias_z)):
                eng.dma_start(dst, src).then_inc(const_ld, 16)
            for n, store in enumerate((*v_st, *x1_st, *y_st)):
                eng.dma_start(opening[:, n, :], bias_o).then_inc(store, 16)

            def load_s(b, i, j):
                at = eng.snap((i * 2 + j) * BP)
                p = eng.snap(b * PAIRS + i)
                eng.wait_ge(st_used[j], p + 1)
                alone(eng)
                eng.dma_start(xs[j][:, :, :], x_v[bass.ds(b, 1), :, :, bass.ds(at, BP)]
                              .rearrange("a p c n -> (a p) c n")).then_inc(st_ld[j], 16)

            def load_a(b, i, j):
                at = eng.snap((i * 2 + j) * BP)
                p = eng.snap(b * PAIRS + i)
                eng.wait_ge(row_full[j][ROWS - 1], p + 1)
                alone(eng)
                eng.dma_start(xa[j][:, :, :], x_v[bass.ds(b, 1), :, :, bass.ds(at, BP)]
                              .rearrange("a p c n -> (a p) c n")).then_inc(xa_ld[j], 16)

            def load_r(b, i, j):
                at = eng.snap((i * 2 + j) * BP)
                p = eng.snap(b * PAIRS + i)
                eng.wait_ge(psG_full[j], p + 1)
                alone(eng)
                eng.wait_ge(x1_st[j], (b * PAIRS + i) * 16 + 16)
                alone(eng)
                eng.dma_start(xr[j][:, :, :], x_v[bass.ds(b, 1), :, :, bass.ds(at, BP)]
                              .rearrange("a p c n -> (a p) c n")).then_inc(xr_ld[j], 16)

            def image(g, a, s):
                with eng.Fori(0, PAIRS) as i:
                    for j in range(2):
                        if a is not None:
                            load_a(a, i, j)
                        if s is not None:
                            load_s(s, i, j)
                        if g is not None:
                            load_r(g, i, j)

            run(eng, image)
            for j in range(2):
                eng.wait_ge(psG_full[j], B * PAIRS + 1)
                eng.wait_ge(x1_st[j], B * PAIRS * 16 + 16)
            with eng.Fori(0, B) as b:
                with eng.Fori(0, PIX // YB // NY) as i:
                    for j in range(NY):
                        at = eng.snap((i * NY + j) * YB)
                        eng.wait_ge(y_st[j], (b * (PIX // YB // NY) + i) * 16 + 16)
                        alone(eng)
                        eng.dma_start(y_buf[j], x1_v[bass.ds(b, 1), :, :, bass.ds(at, YB)]
                                      .rearrange("a p c n -> (a p) c n")).then_inc(y_ld[j], 16)
            for j in range(NY):
                eng.wait_ge(y_st[j], B * (PIX // YB // NY) * 16 + 16)
            for j in range(2):
                eng.wait_ge(v_st[j], B * PAIRS * 16 + 16)

        @block.vector
        def _(eng):
            eng.memset(taps[:, :, :], 0.0).then_inc(setup_v, 1)
            eng.memset(x1T[:, :, :, :], 1.0).then_inc(setup_v, 1)
            eng.memset(gram[:, :, :, :], 0.0).then_inc(setup_v, 1)
            eng.memset(carry[0][:, :, :], 0.0).then_inc(setup_v, 1)
            eng.memset(carry[1][:, :, :], 0.0).then_inc(setup_v, 1)
            eng.wait_ge(consts, 11)
            eng.wait_ge(const_ld, 16 * 7)
            eng.wait_ge(setup_v, 5)
            eng.tensor_tensor(grid[:, :, :], grid[:, :, :],
                              off_b[:, 0:2 * G].unsqueeze(1).to_broadcast([P, H, 2 * G]), ALU.add)\
               .then_inc(setup_v, 1)
            eng.tensor_scalar(first_patch[:, :, :], first_patch[:, :, :], float(W * ENT), None, ALU.mult)\
               .then_inc(setup_v, 1)
            eng.wait_ge(setup_v, 7)

            def take_stats(b, i, j):
                eng.wait_ge(st_ld[j], (b * PAIRS + i) * 16 + 16)
                for c in range(CC):
                    ins = eng.bn_stats(bst[:, c, bass.ds(i * 2 + j, 1), :]
                                       .rearrange("p a s -> p (a s)"), xs[j][:, c, :])
                ins.then_inc(st_used[j], 1)

            NS = 7

            def prep(b):
                count = 0

                def step(ins):
                    nonlocal count
                    count += 1
                    ins.then_inc(st_v, 1)
                    eng.wait_ge(st_v, b * NS + count)

                for j in range(2):
                    eng.wait_ge(st_used[j], (b + 1) * PAIRS + 1)
                if not isinstance(b, int):
                    alone(eng)
                for c in range(CC):
                    agg = eng.bn_aggr(mv[:, c, :], bst[:, c, :, :].rearrange("p n s -> p (n s)"))
                step(agg)
                step(eng.tensor_tensor(msq[:, :], mv[:, :, 0], mv[:, :, 0], ALU.mult))
                step(eng.tensor_tensor(mv[:, :, 1], mv[:, :, 1], msq[:, :], ALU.add))
                eng.wait_ge(psI_full, b * NU + 1)
                pg = psI[:, 0:CC * 2].rearrange("p (c k) -> p c k", k=2)
                step(eng.tensor_copy(mean_x[:, :], pg[:, :, 0]))
                step(eng.tensor_tensor(msq[:, :], mean_x[:, :], mean_x[:, :], ALU.mult))
                eng.tensor_tensor(rstd_x[:, :], pg[:, :, 1], msq[:, :], ALU.subtract)\
                   .then_inc(psI_free, 1)
                eng.wait_ge(psI_free, b * NU + 2)
                step(eng.tensor_scalar(rstd_x[:, :], rstd_x[:, :], 0.0, EPS_GN, ALU.max, ALU.add))
                eng.wait_ge(st_a, b + 1)
                step(eng.reciprocal(rstd_x[:, :], rstd_x[:, :]))
                assert count == NS
                for c in range(CC):
                    eng.tensor_scalar(wB[:, c, :], wA_sb[:, c, :], rstd_x[:, c:c + 1],
                                      None, ALU.mult).then_inc(w_ready, 1)
                    eng.tensor_copy(mean_bc[:, c, :], mean_x[:, c:c + 1].to_broadcast([P, P]))\
                       .then_inc(w_ready, 1)
                eng.wait_ge(psI_full, b * NU + 2)
                eng.tensor_tensor(biasB[:, :], biasA_sb[:, :], psI[:, 0:NA], ALU.subtract)\
                   .then_inc(psI_free, 1)
                eng.wait_ge(psI_free, b * NU + 3)

            def conv_out(b, i, j, rows):
                for r in rows:
                    k = r % 2
                    eng.wait_ge(row_full[j][r], b * PAIRS + i + 2)
                    if r == 0:
                        eng.wait_ge(v_st[j], (b * PAIRS + i) * 16 + 16)
                    if r == ROWS - 1:
                        eng.wait_ge(v_dup, (b * PAIRS + i) * 10 + 5 * j + 2)
                    dst = vring[j][:, r + 1, :, 0, :] if r < ROWS - 1 else carry[j][:, :, :]
                    eng.tensor_tensor(dst, psA[k][:, 0:C].rearrange("p (g e) -> p g e", g=G),
                                      biasB[:, 0:C].rearrange("p (g e) -> p g e", g=G), ALU.add)\
                       .then_inc(v_row, 1)
                    eng.tensor_tensor(taps[:, bass.ds((i * 2 + j) * ROWS + r + 1, 1), :]
                                      .rearrange("p a n -> p (a n)"),
                                      psA[k][:, C:NA], biasB[:, C:NA], ALU.add)\
                       .then_inc(psA_free[k], 1)

            NV = 18

            def place(b, q):
                ix, a, bb, m0, m1 = (pt[n][:, :, :] for n in ("ix", "a", "b", "m0", "m1"))
                tm, th, w0, w1, ia = (pm[n][:, :, :] for n in ("tm", "th", "w0", "w1", "ia"))
                pq = psI[:, 0:QR * NO].rearrange("p (r o) -> p r o", o=NO)
                base = (b * NQ + q) * NV
                count = 0

                def step(ins):
                    nonlocal count
                    count += 1
                    ins.then_inc(place_v, 1)
                    eng.wait_ge(place_v, base + count)

                eng.wait_ge(psI_full, b * NU + 3 + q)
                eng.tensor_tensor(tm, pq[:, :, 2 * G:NO],
                                  off_b[:, 2 * G:NO].unsqueeze(1).to_broadcast([P, QR, G]),
                                  ALU.add).then_inc(mod_in, 1)
                eng.tensor_tensor(a, pq[:, :, 0:2 * G], grid[:, bass.ds(q * QR, QR), :],
                                  ALU.add).then_inc(psI_free, 1)
                eng.wait_ge(psI_free, b * NU + q + 4)
                step(eng.tensor_scalar(ix, a, W / (W - 1.0), 0.5, ALU.mult, ALU.subtract))
                step(eng.tensor_scalar(a, ix, 0.5, 0.0, ALU.subtract, ALU.max))
                step(eng.tensor_scalar(a, a, W - 2.0, MAGIC, ALU.min, ALU.add))
                step(eng.tensor_scalar(a, a, MAGIC, None, ALU.subtract))
                step(eng.tensor_tensor(ix, ix, a, ALU.subtract))
                step(eng.tensor_scalar(bb, ix, -1.0, 1.0, ALU.mult, ALU.add))
                step(eng.scalar_tensor_tensor(m0, ix, 1.0, bb, ALU.add, ALU.min))
                step(eng.tensor_scalar(bb, bb, 1.0, None, ALU.add))
                step(eng.tensor_tensor(m1, ix, bb, ALU.min))
                step(eng.scalar_tensor_tensor(ia, a[:, :, 0:G], float(ENT), first_patch[:, :, :],
                                              ALU.mult, ALU.add))
                step(eng.scalar_tensor_tensor(
                    index[:, bass.ds(q * (QR * G), QR * G)].rearrange("p (r g) -> p r g", g=G),
                    a[:, :, G:2 * G], float(VROW), ia, ALU.mult, ALU.add))
                eng.wait_ge(mod_out, b * NQ + q + 1)
                step(eng.tensor_scalar(th, th, 1.0, None, ALU.add))
                step(eng.scalar_tensor_tensor(w0, m0[:, :, G:2 * G], 0.0, th, ALU.max, ALU.mult))
                step(eng.scalar_tensor_tensor(w1, m1[:, :, G:2 * G], 0.0, th, ALU.max, ALU.mult))
                wv = weight[:, bass.ds(q * (QR * G * 4), QR * G * 4)]\
                    .rearrange("p (r g k) -> p r g k", g=G, k=4)
                for k, (mx, wy) in enumerate(((m0, w0), (m0, w1), (m1, w0), (m1, w1))):
                    step(eng.scalar_tensor_tensor(wv[:, :, :, k], mx[:, :, 0:G], 0.0, wy,
                                                  ALU.max, ALU.mult))
                assert count == NV
                eng.sem_inc(placed, 1)

            def sample(b, i, j, h):
                eng.wait_ge(got[j][h], (b * PAIRS + i) * (NH * 16) + NH * 16)
                mine = patch[j][:, h * NH:(h + 1) * NH, :]
                v4 = mine.rearrange("p t (k e) -> p (t k) e", e=CG)
                w4 = weight[:, bass.ds(((i * 2 + j) * 2 + h) * (NH * 4), NH * 4)].unsqueeze(2)\
                    .to_broadcast([P, NH * 4, CG])
                eng.tensor_tensor(v4, v4, w4, ALU.mult).then_inc(weighted, 1)
                eng.wait_ge(weighted, (b * PAIRS + i) * 4 + 2 * j + h + 1)
                eng.tensor_tensor(mine[:, :, 0:ENT], mine[:, :, 0:ENT], mine[:, :, ENT:PATCH],
                                  ALU.add).then_inc(halved, 1)
                eng.wait_ge(halved, (b * PAIRS + i) * 4 + 2 * j + h + 1)
                eng.tensor_tensor(samp[j][:, 2 * h:2 * h + 2, :].rearrange("p r (g e) -> p (r g) e", g=G),
                                  mine[:, :, 0:CG], mine[:, :, CG:ENT], ALU.add)\
                   .then_inc(sampled[j][h], 1)

            def residual(b, i, j):
                eng.wait_ge(xr_ld[j], (b * PAIRS + i) * 16 + 16)
                for o in range(CC):
                    eng.wait_ge(psO_full[o], (b * PAIRS + i) * 2 + j + 2)
                    eng.scalar_tensor_tensor(xr[j][:, o, :], psO[o][:, :], bo_sb[:, o:o + 1],
                                             xr[j][:, o, :], ALU.add, ALU.add)\
                       .then_inc(psO_free[o], 1)

            def gram_add(b, i, j):
                eng.wait_ge(psG_full[j], b * PAIRS + i + 2)
                eng.wait_ge(psG_free, (b * PAIRS + i) * 2 + j + 1)
                gb = gram[:, bass.ds(b, 1), :, :].rearrange("p a c n -> p (a c n)")
                eng.tensor_tensor(gb, gb, psG[:, 0:CC * (P + 1)], ALU.add).then_inc(psG_free, 1)

            def image(g, a, s):
                if a is not None:
                    prep(a)

                def pair(i):
                    first = isinstance(i, int) and i == 0
                    for j in range(2):
                        if g is not None:
                            sample(g, i, j, 0)
                        if a is not None:
                            conv_out(a, i, j, (0, 1))
                        if g is not None:
                            sample(g, i, j, 1)
                            if j == 1:
                                gram_add(g, i, 0)
                            elif not first:
                                gram_add(g, i - 1, 1)
                        if a is not None:
                            conv_out(a, i, j, (2, 3))
                        if s is not None:
                            take_stats(s, i, j)
                        if a is not None and j == 1 and not first:
                            place(a, i - 1)
                        if g is not None:
                            residual(g, i, j)

                pairs(eng, pair)
                if a is not None:
                    place(a, PAIRS - 1)
                if g is not None:
                    gram_add(g, PAIRS - 1, 1)

            run(eng, image)

            done = 0

            def step(ins):
                nonlocal done
                done += 1
                ins.then_inc(wh_v, 1)
                eng.wait_ge(wh_v, done)

            eng.wait_ge(psG_free, B * BLOCKS + 1)
            step(eng.tensor_copy(sums, gram[:, :, :, P:P + 1].rearrange("p b c n -> p c (b n)")))
            step(eng.tensor_scalar(st2[:, :, :, 0], sums, 1.0 / PIX, None, ALU.mult))
            for c in range(CC):
                step(eng.tensor_tensor(scr[:, c, :, :], gram[:, :, c, 0:P],
                                       ident[:, :].unsqueeze(1).to_broadcast([P, B, P]), ALU.mult))
            step(eng.tensor_reduce(var, scr, AX_X, ALU.add))
            step(eng.tensor_scalar(st2[:, :, :, 1], var, 1.0 / PIX, None, ALU.mult))
            mark["w_channels"] = done
            eng.wait_ge(wh_p, P_STATS)
            pg = psI[:, 0:CC * B * 2].rearrange("p (c b k) -> p c b k", b=B, k=2)
            step(eng.tensor_copy(gm, pg[:, :, :, 0]))
            step(eng.tensor_tensor(var, gm, gm, ALU.mult))
            step(eng.tensor_tensor(var, pg[:, :, :, 1], var, ALU.subtract))
            step(eng.tensor_scalar(var, var, 0.0, EPS_GN, ALU.max, ALU.add))
            mark["w_variance"] = done
            eng.wait_ge(wh_a, 1)
            step(eng.reciprocal(rs, var))
            step(eng.tensor_tensor(g_b, gm, rs, ALU.mult))
            step(eng.tensor_tensor(a_b, sums, rs, ALU.mult))
            step(eng.scalar_tensor_tensor(d_b, g_b, float(PIX), a_b, ALU.mult, ALU.subtract))
            step(eng.tensor_reduce(mu, d_b, AX_X, ALU.add))
            step(eng.tensor_scalar(mu, mu, -1.0 / (B * PIX), None, ALU.mult))
            for c in range(CC):
                for b in range(B):
                    step(eng.tensor_scalar(scr[:, c, b, :], gram[:, b, c, 0:P], rs[:, c, b:b + 1],
                                           None, ALU.mult))
            mark["w_scaled"] = done
            for c in range(CC):
                eng.wait_ge(wh_p, P_ROWS + c)
                step(eng.tensor_copy(rowsT[0:B, c, 0, :], psT[c][0:B, 0:P]))
                step(eng.tensor_scalar(rowsT[0:B, c, 1, :], psT[c][0:B, P:2 * P], -1.0, None, ALU.mult))
                step(eng.tensor_copy(rowsT[0:B, c, 2, :], psT[c][0:B, 2 * P:3 * P]))
                step(eng.tensor_copy(rowsT[0:1, c, 3, :], psT[c][0:1, 3 * P:4 * P]))
                step(eng.tensor_scalar(T[0:1, c, :], rowsT[0:1, c, 3, :], -float(B * PIX), None,
                                       ALU.mult))
            mark["w_rows"] = done
            for c in range(CC):
                for b in range(B):
                    n = c * B + b
                    eng.wait_ge(wh_p, P_GRAM + n)
                    if b == 0:
                        step(eng.tensor_scalar(cov[:, c, :], psA[n % 2][:, 0:P], rs[:, c, b:b + 1],
                                               None, ALU.mult))
                    else:
                        step(eng.scalar_tensor_tensor(cov[:, c, :], psA[n % 2][:, 0:P],
                                                      rs[:, c, b:b + 1], cov[:, c, :],
                                                      ALU.mult, ALU.add))
            for c in range(CC):
                eng.wait_ge(wh_p, P_CROSS + c)
                step(eng.tensor_tensor(cov[:, c, :], cov[:, c, :], psO[c][:, 0:P], ALU.add))
                step(eng.scalar_tensor_tensor(cov[:, c, :], cov[:, c, :], 1.0 / (B * PIX),
                                              same16[:, :], ALU.mult, ALU.mult))
                step(eng.scalar_tensor_tensor(cov[:, c, :], ident[:, :], EPS_Z, cov[:, c, :],
                                              ALU.mult, ALU.add))
                step(eng.tensor_tensor(Y[:, c, :], cov[:, c, :], ident[:, :], ALU.mult))
            step(eng.tensor_reduce(tr, Y, AX_X, ALU.add))
            mark["w_trace"] = done
            eng.wait_ge(wh_p, P_TRACE)
            step(eng.tensor_copy(tr, psI[:, 0:CC]))
            mark["w_root"] = done
            step(eng.reciprocal(rtr, tr))
            for c in range(CC):
                step(eng.tensor_scalar(Y[:, c, :], cov[:, c, :], rtr[:, c:c + 1], None, ALU.mult))
                step(eng.tensor_copy(Z[:, c, :], ident[:, :]))
            step(eng.tensor_scalar(i15, ident[:, :], 1.5, None, ALU.mult))
            eng.sem_inc(ns_new, 1)
            with eng.Fori(0, STEPS) as s:
                for c in range(CC):
                    eng.wait_ge(ns_zy, s * CC + c + 1)
                    eng.scalar_tensor_tensor(T[:, c, :], psA[c][:, 0:P], -0.5, i15, ALU.mult,
                                             ALU.add).then_inc(ns_t, 1)
                for c in range(CC):
                    eng.wait_ge(ns_zt, s * CC + c + 1)
                    eng.tensor_copy(Y[:, c, :], psT[c][:, 0:P])
                    ins = eng.tensor_copy(Z[:, c, :], psO[c][:, 0:P])
                ins.then_inc(ns_new, 1)
            eng.wait_ge(ns_new, STEPS + 1)
            eng.wait_ge(wh_a, 2)
            step(eng.reciprocal(srt, srt))
            for c in range(CC):
                step(eng.tensor_scalar(dg[:, c, :], ident[:, :], wz_sb[:, c:c + 1], None, ALU.mult))
            mark["w_root_of_cov"] = done
            for c in range(CC):
                eng.wait_ge(wh_p, P_PW + c)
                step(eng.tensor_scalar(pw[:, c, :], psA[c][:, 0:P], srt[:, c:c + 1], None, ALU.mult))
                step(eng.tensor_scalar(gmu[:, c, :], g_b[:, c, :], mu[:, c:c + 1], None, ALU.add))
            mark["w_pw"] = done
            for c in range(CC):
                eng.wait_ge(wh_p, P_CST + CC - 1)
                step(eng.tensor_scalar(cst[:, c, :], psG[:, c * B:(c + 1) * B], -1.0,
                                       bz_sb[:, c:c + 1], ALU.mult, ALU.add))
            with eng.Fori(0, B) as b:
                for j in range(NY):
                    eng.wait_ge(y_add[j], b * (PIX // YB // NY) + 1)
                for c in range(CC):
                    eng.tensor_scalar(amap[:, c, :], pw[:, c, :], rs[:, c, bass.ds(b, 1)], None,
                                      ALU.mult).then_inc(map_v, 1)
                    eng.tensor_copy(cnow[:, c:c + 1], cst[:, c, bass.ds(b, 1)]).then_inc(map_v, 1)
                eng.wait_ge(map_v, (b + 1) * (2 * CC))
                alone(eng)
                with eng.Fori(0, PIX // YB // NY) as i:
                    for j in range(NY):
                        eng.wait_ge(y_mm[j], b * (PIX // YB // NY) + i + 1)
                        for k in range(CC * YB // 512):
                            c, at = k // (YB // 512), k % (YB // 512) * 512
                            part = y_buf[j][:, c, at:at + 512]
                            ins = eng.scalar_tensor_tensor(part, y_bank[j % 2][k][:, :],
                                                           cnow[:, c:c + 1], part, ALU.add, ALU.add)
                        ins.then_inc(y_add[j], 1)

        @block.gpsimd
        def _(eng):
            for free in (*st_used, *row_full[0], *row_full[1], *sampled[0], *sampled[1], *psT_free, *psO_free,
                         *psO_full, *psG_full, psG_free, *psA_free, psI_free, v_dup, *y_add):
                eng.sem_inc(free, 1)
            eng.memset(ident[:, :], 0.0).then_inc(zeros, 1)
            eng.memset(shift[:, :, :], 0.0).then_inc(zeros, 1)
            eng.memset(avg8[:, :], 1.0 / GN1).then_inc(zeros, 1)
            eng.memset(same16[:, :], 1.0).then_inc(zeros, 1)
            eng.wait_ge(zeros, 4)
            eng.affine_select(out=ident[:, :], in_=ident[:, :], compare_op=ALU.not_equal, fill=1.0,
                              base=0, pattern=[[-1, P]], channel_multiplier=1).then_inc(consts, 1)
            for d in range(3):
                eng.affine_select(out=shift[:, d, :], in_=shift[:, d, :], compare_op=ALU.not_equal,
                                  fill=1.0, base=1 - d, pattern=[[-1, P]],
                                  channel_multiplier=1).then_inc(consts, 1)
            done = 4
            for m, g in ((avg8, GN1), (same16, GZ)):
                eng.affine_select(out=m[:, :], in_=m[:, :], compare_op=ALU.is_ge, fill=0.0, base=0,
                                  pattern=[[-g, P // g], [0, g]],
                                  channel_multiplier=1).then_inc(consts, 1)
                done += 1
                eng.wait_ge(consts, done)
                eng.affine_select(out=m[:, :], in_=m[:, :], compare_op=ALU.is_ge, fill=0.0,
                                  base=g - 1, pattern=[[g, P // g], [0, g]],
                                  channel_multiplier=-1).then_inc(consts, 1)
                done += 1
            eng.iota(grid[:, :, 0:G], pattern=[[0, H], [0, G]], base=0, channel_multiplier=1,
                     allow_small_or_imprecise_dtypes=True).then_inc(consts, 1)
            eng.iota(grid[:, :, G:2 * G], pattern=[[1, H], [0, G]], base=0, channel_multiplier=0,
                     allow_small_or_imprecise_dtypes=True).then_inc(consts, 1)
            eng.iota(first_patch[:, :, :], pattern=[[0, QR], [1, G]], base=G, channel_multiplier=0,
                     allow_small_or_imprecise_dtypes=True).then_inc(consts, 1)

            def gather(b, k, i, j):
                eng.wait_ge(sampled[j][1], b * PAIRS + i + 1)
                eng.wait_ge(index_cp, (b * PAIRS + i) * 2 + j + 1)
                alone(eng)
                for t in range(NJ):
                    eng.indirect_dma_start(
                        out=patch[j][:, t, :], out_offset=None, in_=v2_flat[k],
                        in_offset=bass.IndirectOffsetOnAxis(ap=index_now[j][:, t:t + 1], axis=1),
                    ).then_inc(got[j][t // NH], 16)

            with eng.Fori(0, B // 2) as h:
                for k in range(2):
                    b = h * 2 + k
                    for j in range(2):
                        eng.wait_ge(v_st[j], (b + 1) * (PAIRS * 16) + 16)
                    alone(eng)
                    with eng.Fori(0, PAIRS) as i:
                        for j in range(2):
                            gather(b, k, i, j)

        def whiten_tensor(eng):
            eng.wait_ge(wh_v, mark["w_channels"])
            eng.matmul(psI[:, 0:CC * B * 2], avg8[:, :],
                       st2.rearrange("p c b k -> p (c b k)"), start=True, stop=True)\
               .then_inc(wh_p, 1)
            eng.wait_ge(wh_v, mark["w_scaled"])
            for c in range(CC):
                for k, m in enumerate((g_b, a_b, d_b)):
                    eng.matmul(psT[c][0:B, k * P:(k + 1) * P], m[:, c, :], ident[:, :],
                               start=True, stop=True)
                eng.matmul(psT[c][0:1, 3 * P:4 * P], mu[:, c:c + 1], ident[:, :],
                           start=True, stop=True).then_inc(wh_p, 1)
            for c in range(CC):
                for b in range(B):
                    n = c * B + b
                    if n >= 2:
                        eng.wait_ge(wh_v, mark["w_rows"] + n - 1)
                    eng.matmul(psA[n % 2][:, 0:P], scr[:, c, b, :], ident[:, :],
                               start=True, stop=True).then_inc(wh_p, 1)
            eng.wait_ge(wh_v, mark["w_rows"])
            for c in range(CC):
                eng.matmul(psO[c][:, 0:P], rowsT[0:B, c, 1, :], rowsT[0:B, c, 0, :],
                           start=True, stop=False)
                eng.matmul(psO[c][:, 0:P], rowsT[0:B, c, 0, :], rowsT[0:B, c, 2, :],
                           start=False, stop=False)
                eng.matmul(psO[c][:, 0:P], rowsT[0:1, c, 3, :], T[0:1, c, :],
                           start=False, stop=True).then_inc(wh_p, 1)
            eng.wait_ge(wh_v, mark["w_trace"])
            eng.matmul(psI[:, 0:CC], same16[:, :], tr, start=True, stop=True).then_inc(wh_p, 1)
            with eng.Fori(0, STEPS) as s:
                eng.wait_ge(ns_new, s + 1)
                for c in range(CC):
                    eng.matmul(psA[c][:, 0:P], Z[:, c, :], Y[:, c, :], start=True, stop=True)\
                       .then_inc(ns_zy, 1)
                for c in range(CC):
                    eng.wait_ge(ns_t, s * CC + c + 1)
                    eng.matmul(psT[c][:, 0:P], Y[:, c, :], T[:, c, :], start=True, stop=True)
                    eng.matmul(psO[c][:, 0:P], T[:, c, :], Z[:, c, :], start=True, stop=True)\
                       .then_inc(ns_zt, 1)
            eng.wait_ge(wh_v, mark["w_root_of_cov"])
            for c in range(CC):
                eng.matmul(psA[c][:, 0:P], Z[:, c, :], dg[:, c, :], start=True, stop=True)\
                   .then_inc(wh_p, 1)
            eng.wait_ge(wh_v, mark["w_pw"])
            for c in range(CC):
                eng.matmul(psG[:, c * B:(c + 1) * B], pw[:, c, :], gmu[:, c, :],
                           start=True, stop=True).then_inc(wh_p, 1)

        @block.tensor
        def _(eng):
            eng.wait_ge(consts, 11)
            eng.wait_ge(const_ld, 16 * 7)
            def prep(b):
                eng.wait_ge(st_v, b * 7 + 3)
                eng.wait_ge(psI_free, b * NU + 1)
                eng.matmul(psI[:, 0:CC * 2], avg8[:, :], mv[:, :, :].rearrange("p c k -> p (c k)"),
                           start=True, stop=True).then_inc(psI_full, 1)
                eng.wait_ge(w_ready, (b + 1) * 4)
                eng.wait_ge(psI_free, b * NU + 2)
                for c in range(CC):
                    mm = eng.matmul(psI[:, 0:NA], mean_bc[:, c, :], wB[:, c, :],
                                    start=(c == 0), stop=(c == CC - 1))
                mm.then_inc(psI_full, 1)

            def conv_rows(b, i, j, rows):
                if 0 in rows:
                    eng.wait_ge(xa_ld[j], (b * PAIRS + i) * 16 + 16)
                for r in rows:
                    k = r % 2
                    eng.wait_ge(psA_free[k], (b * PAIRS + i) * 4 + 2 * j + r // 2 + 1)
                    for c in range(CC):
                        mm = eng.matmul(psA[k][:, 0:NA], xa[j][:, c, r * W:(r + 1) * W],
                                        wB[:, c, :], start=(c == 0), stop=(c == CC - 1))
                    mm.then_inc(row_full[j][r], 1)

            def offsets(b, q):
                last = isinstance(q, int) and q == PAIRS - 1
                for k in range(2):
                    eng.wait_ge(psA_free[k], (b * PAIRS + q) * 4 + 5 + (0 if last else 2))
                eng.wait_ge(psI_free, b * NU + q + 3)
                for t in range(NTAP):
                    dy, dx = t // 3, t % 3
                    mm = eng.matmul(psI[:, 0:QR * NO].rearrange("p (r o) -> p r o", o=NO),
                                    shift[:, dx, :],
                                    taps[:, bass.ds(q * QR + dy, QR), t * NO:(t + 1) * NO],
                                    start=(t == 0), stop=(t == NTAP - 1))
                mm.then_inc(psI_full, 1)

            def turn_samples(b, i, j, h):
                eng.wait_ge(sampled[j][h], b * PAIRS + i + 2)
                for c in range(CC):
                    if h == 0:
                        eng.wait_ge(psT_free[c], (b * PAIRS + i) * 4 + 2 * j + 1)
                    for r in (2 * h, 2 * h + 1):
                        mm = eng.transpose(psT[c][:, r * W:(r + 1) * W],
                                           samp[j][:, r, c * P:(c + 1) * P], ident[:, :])
                    if h == 1:
                        mm.then_inc(psT_full[c], 1)

            def out_conv(b, i, j):
                for h in range(CC):
                    eng.wait_ge(psT_free[h], (b * PAIRS + i) * 4 + 2 * j + 2)
                for o in range(CC):
                    eng.wait_ge(psO_free[o], (b * PAIRS + i) * 2 + j + 1)
                    for h in range(CC):
                        mm = eng.matmul(psO[o][:, :], wO_sb[:, h, o * P:(o + 1) * P],
                                        sampT[:, h, :], start=(h == 0), stop=(h == CC - 1))
                    mm.then_inc(psO_full[o], 1)

            def turn_x1(b, i, j):
                for o in range(CC):
                    eng.wait_ge(psO_free[o], (b * PAIRS + i) * 2 + j + 2)
                for h in range(2):
                    eng.wait_ge(psT_free[h], (b * PAIRS + i) * 4 + 2 * j + 2)
                    for r in range(2):
                        for c in range(CC):
                            at = (r * CC + c) * P
                            row = 2 * h + r
                            mm = eng.transpose(psT[h][:, at:at + P],
                                               xr[j][:, c, row * W:(row + 1) * W], ident[:, :])
                    mm.then_inc(psT_full[h], 1)

            def gram_block(b, i, j):
                for h in range(2):
                    eng.wait_ge(psT_free[h], (b * PAIRS + i) * 4 + 2 * j + 3)
                eng.wait_ge(psG_free, (b * PAIRS + i) * 2 + j + 1)
                for c in range(CC):
                    for r in range(ROWS):
                        mm = eng.matmul(psG[:, c * (P + 1):(c + 1) * (P + 1)], x1T[:, r, c, 0:P],
                                        x1T[:, r, c, :], start=(r == 0), stop=(r == ROWS - 1))
                mm.then_inc(psG_full[j], 1)

            def image(g, a, s):
                if a is not None:
                    prep(a)

                def pair(i):
                    first = isinstance(i, int) and i == 0
                    for j in range(2):
                        def conv(rows):
                            if a is not None:
                                conv_rows(a, i, j, rows)

                        def before(part):
                            if j == 1:
                                part(g, i, 0)
                            elif not first:
                                part(g, i - 1, 1)

                        if g is None:
                            conv(range(ROWS))
                            if j == 1 and not first:
                                offsets(a, i - 1)
                        else:
                            conv((0,))
                            before(turn_x1)
                            conv((1,))
                            if a is not None and j == 1 and not first:
                                offsets(a, i - 1)
                            before(gram_block)
                            turn_samples(g, i, j, 0)
                            conv((2, 3))
                            turn_samples(g, i, j, 1)
                            out_conv(g, i, j)

                if a is not None or g is not None:
                    pairs(eng, pair)
                if a is not None:
                    offsets(a, PAIRS - 1)
                if g is not None:
                    turn_x1(g, PAIRS - 1, 1)
                    gram_block(g, PAIRS - 1, 1)

            run(eng, image)
            whiten_tensor(eng)
            with eng.Fori(0, B) as b:
                eng.wait_ge(map_v, (b + 1) * (2 * CC))
                alone(eng)
                with eng.Fori(0, PIX // YB // NY) as i:
                    for j in range(NY):
                        eng.wait_ge(y_ld[j], (b * (PIX // YB // NY) + i) * 16 + 16)
                        if j < 2:
                            eng.wait_ge(y_add[j + NY - 2], b * (PIX // YB // NY) + i + 1)
                        else:
                            eng.wait_ge(y_add[j - 2], b * (PIX // YB // NY) + i + 2)
                        for k in range(CC * YB // 512):
                            c, at = k // (YB // 512), k % (YB // 512) * 512
                            mm = eng.matmul(y_bank[j % 2][k][:, :], amap[:, c, :],
                                            y_buf[j][:, c, at:at + 512], start=True, stop=True)
                        mm.then_inc(y_mm[j], 1)

        @block.scalar
        def _(eng):
            def root(b):
                eng.wait_ge(st_v, b * 7 + 6)
                eng.activation(rstd_x[:, :], rstd_x[:, :], ACT.Sqrt).then_inc(st_a, 1)

            def dup(b, i, j, rows):
                for r in rows:
                    src = vring[j][:, r + 1, :, 0, :] if r < ROWS - 1 else carry[j][:, :, :]
                    eng.wait_ge(v_row, (b * PAIRS + i) * 8 + 4 * j + r + 1)
                    if r == 0:
                        eng.activation(vring[j][:, 0, :, 0, :], carry[1 - j][:, :, :], ACT.Copy)\
                           .then_inc(v_dup, 1)
                    eng.activation(vring[j][:, r, :, 1, :], src, ACT.Copy).then_inc(v_dup, 1)

            def v_store(b, k, i, j):
                row = eng.snap((i * 2 + j) * NJ)
                eng.wait_ge(v_dup, (b * PAIRS + i) * 10 + 5 * j + 6)
                eng.dma_start(v2_rows[k][:, bass.ds(row, NJ), :],
                              vring[j][:, :, :, :, :].rearrange("p r g k e -> p (r g) (k e)"))\
                   .then_inc(v_st[j], 16)

            def samples_out(b, i, j):
                eng.wait_ge(psO_full[CC - 1], (b * PAIRS + i) * 2 + j + 1)
                for h in range(CC):
                    eng.wait_ge(psT_full[h], (b * PAIRS + i) * 4 + 2 * j + 1)
                    eng.activation(sampT[:, h, :], psT[h][:, :], ACT.Copy).then_inc(psT_free[h], 1)

            def x1_store(b, i, j):
                at = eng.snap((i * 2 + j) * BP)
                bb = eng.snap(b) if not isinstance(b, int) else b
                for o in range(CC):
                    eng.wait_ge(psO_free[o], (b * PAIRS + i) * 2 + j + 2)
                eng.dma_start(x1_v[bass.ds(bb, 1), :, :, bass.ds(at, BP)]
                              .rearrange("a p c n -> (a p) c n"), xr[j][:, :, :])\
                   .then_inc(x1_st[j], 16)

            def x1_out(b, i, j):
                eng.wait_ge(psG_full[1 - j], b * PAIRS + i + j + 1)
                for h in range(2):
                    eng.wait_ge(psT_full[h], (b * PAIRS + i) * 4 + 2 * j + 2)
                    eng.activation(x1T[:, 2 * h:2 * h + 2, :, 0:P].rearrange("p r c n -> p (r c) n"),
                                   psT[h][:, :].rearrange("p (q n) -> p q n", n=P), ACT.Copy)\
                       .then_inc(psT_free[h], 1)

            def indices(b, n, i, j):
                eng.wait_ge(sampled[j][1], b * PAIRS + n + 1)
                eng.activation(index_now[j][:, :], index[:, bass.ds((i * 2 + j) * NJ, NJ)], ACT.Copy)\
                   .then_inc(index_cp, 1)

            def modulation(b, q):
                eng.wait_ge(mod_in, b * NQ + q + 1)
                eng.activation(pm["th"][:, :, :], pm["tm"][:, :, :], ACT.Tanh).then_inc(mod_out, 1)

            def image(g, a, k):
                if g is not None:
                    eng.wait_ge(placed, (g + 1) * NQ)
                    for j in range(2):
                        indices(g, 0, 0, j)
                if a is not None:
                    root(a)

                def pair(i):
                    first = isinstance(i, int) and i == 0
                    last = isinstance(i, int) and i == PAIRS - 1
                    for j in range(2):
                        if g is not None:
                            if j == 1:
                                x1_out(g, i, 0)
                            elif not first:
                                x1_out(g, i - 1, 1)
                        if a is not None:
                            dup(a, i, j, (0, 1))
                        if g is not None:
                            samples_out(g, i, j)
                            if not last:
                                indices(g, i + 1, i + 1, j)
                        if a is not None:
                            dup(a, i, j, (2, 3))
                            v_store(a, k, i, j)
                            if j == 1 and not first:
                                modulation(a, i - 1)
                        if g is not None:
                            x1_store(g, i, j)

                pairs(eng, pair)
                if a is not None:
                    modulation(a, PAIRS - 1)
                if g is not None:
                    x1_out(g, PAIRS - 1, 1)

            image(None, 0, 0)
            if B > 2:
                with eng.Fori(0, B // 2 - 1) as h:
                    for k in range(2):
                        image(h * 2 + k, h * 2 + k + 1, 1 - k)
            image(B - 2, B - 1, 1)
            image(B - 1, None, None)
            eng.wait_ge(wh_v, mark["w_variance"])
            eng.activation(var, var, ACT.Sqrt).then_inc(wh_a, 1)
            eng.wait_ge(wh_v, mark["w_root"])
            eng.activation(srt, tr, ACT.Sqrt).then_inc(wh_a, 1)
            with eng.Fori(0, B) as b:
                with eng.Fori(0, PIX // YB // NY) as i:
                    for j in range(NY):
                        at = eng.snap((i * NY + j) * YB)
                        eng.wait_ge(y_add[j], b * (PIX // YB // NY) + i + 2)
                        eng.dma_start(out_v[bass.ds(b, 1), :, :, bass.ds(at, YB)]
                                      .rearrange("a p c n -> (a p) c n"), y_buf[j])\
                           .then_inc(y_st[j], 16)


def kernel(x, L0_conv_offset_w, L0_conv_offset_b, L0_conv_mod_w, L0_conv_mod_b, L0_conv_kv_w,
           L0_conv_kv_b, L0_conv_out_w, L0_conv_out_b, L1_conv_weight, L1_conv_bias):
    import numpy as np
    import concourse.bacc as bacc
    from concourse.bass_utils import run_bass_kernel_spmd

    arr = lambda a: np.ascontiguousarray(a)
    B = x.shape[0]
    heads = C // 32
    perm = np.arange(C).reshape(heads // G, G, 32).transpose(1, 0, 2).reshape(-1)
    order = np.arange(2 * G).reshape(G, 2).T.reshape(-1)
    kv_w = np.asarray(L0_conv_kv_w)[C:, :, 0, 0][perm]
    kv_b = np.asarray(L0_conv_kv_b)[C:][perm]
    taps = np.concatenate([np.asarray(L0_conv_offset_w)[order], np.asarray(L0_conv_mod_w)])
    off_b = np.concatenate([np.asarray(L0_conv_offset_b)[order], np.asarray(L0_conv_mod_b)])
    arrays = {
        "x_dram": arr(x),
        "wA_dram": arr(np.concatenate([kv_w.T, taps.transpose(1, 2, 3, 0).reshape(C, NT)], 1)),
        "biasA_dram": arr(np.concatenate([kv_b, np.zeros(NT, kv_b.dtype)])),
        "bias_off_dram": arr(off_b),
        "wO_dram": arr(np.asarray(L0_conv_out_w)[:, :, 0, 0].T[perm]),
        "bias_o_dram": arr(np.asarray(L0_conv_out_b).reshape(CC, P).T),
        "w_z_dram": arr(np.asarray(L1_conv_weight).reshape(CC, P).T),
        "bias_z_dram": arr(np.asarray(L1_conv_bias).reshape(CC, P).T),
    }
    nc = bacc.Bacc("TRN2", target_bir_lowering=False, num_devices=1)
    args = [nc.dram_tensor(n, a.shape, mybir.dt.from_np(a.dtype), kind="ExternalInput").ap()
            for n, a in arrays.items()]
    out = nc.dram_tensor("out_dram", x.shape, F32, kind="ExternalOutput").ap()
    deform_zca_kernel(nc, B, *args, out)
    r = run_bass_kernel_spmd(nc, [arrays], core_ids=[0])
    return r.results[0]["out_dram"]
```

```python
from contextlib import ExitStack

import concourse.bass as bass
from concourse import mybir

ALU = mybir.AluOpType
ACT = mybir.ActivationFunctionType
AX_X = mybir.AxisListType.X
F32 = mybir.dt.float32
U32 = mybir.dt.uint32

P = 128
C, H, W = 256, 128, 128
PIX = H * W
CC = C // P
G = 4
CG = C // G
NTAP = 9
NO = 3 * G
NT = NTAP * NO
NA = C + NT
ROWS = 4
BP = ROWS * W
BLOCKS = H // ROWS
PAIRS = BLOCKS // 2
NJ = ROWS * G
PATCH = 4 * CG
ENT = 2 * CG
VROWS = H
VROW = G * W * ENT
IMG = VROWS * VROW
QR = 2 * ROWS
NQ = H // QR
NH = NJ // 2
S0 = 4 * BP
YB = 2 * BP
NY = 8
GN1 = 8
GZ = 16
EPS_GN, EPS_Z = 1e-5, 1e-4
MAGIC = 12582912.0


def newton_factors():
    low, factors = (EPS_Z / (4 * GZ)) ** 0.5, []
    while low < 1 - 1e-9:
        f = min(2.6, 3 / (1 + low + low * low)) ** 0.5
        factors.append(f)
        low = min(f * r * (3 - (f * r) ** 2) / 2 for r in (low, 1.0))
    return factors


FACTORS = newton_factors()


def deform_zca_kernel(nc, B, x, wA, biasA, bias_off, wO, bias_o, w_z, bias_z, out):
    v2 = [nc.dram_tensor(f"v2_{j}", [IMG], F32, kind="Internal").ap() for j in range(2)]
    x1 = nc.dram_tensor("x1", [B, CC, P, PIX], F32, kind="Internal").ap()
    x_v = x.rearrange("b (c p) h w -> b p c (h w)", p=P)
    out_v = out.rearrange("b (c p) h w -> b p c (h w)", p=P)
    x1_v = x1.rearrange("b c p n -> b p c n")
    v2_flat = [v.rearrange("(a n) -> a n", a=1) for v in v2]
    v2_rows = [v.rearrange("(r x e) -> x r e", x=W, e=ENT) for v in v2]

    ctx = ExitStack()
    with ctx:
        def sb(name, shape, dt=F32):
            return ctx.enter_context(nc.sbuf_tensor(name, shape, dt))

        def ps(name):
            return ctx.enter_context(nc.psum_tensor(name, [P, 512], F32))

        def sem(name):
            return ctx.enter_context(nc.semaphore(name))

        ident = sb("ident", [P, P])
        shift = sb("shift", [P, 3, P])
        avg8 = sb("avg8", [P, P])
        same16 = sb("same16", [P, P])
        wA_sb = sb("wA_sb", [P, CC, NA])
        wO_sb = sb("wO_sb", [P, CC, C])
        biasA_sb = sb("biasA_sb", [P, NA])
        off_b = sb("off_b", [P, NO])
        bo_sb = sb("bo_sb", [P, CC])
        wz_sb = sb("wz_sb", [P, CC])
        bz_sb = sb("bz_sb", [P, CC])
        grid = sb("grid", [P, H, 2 * G])
        first_patch = sb("first_patch", [P, QR, G])
        opening = sb("opening", [P, 4 + NY, CC])
        wB = sb("wB", [P, CC, NA])
        mean_bc = sb("mean_bc", [P, CC, P])
        biasB = sb("biasB", [P, NA])
        taps = sb("taps", [P, H + 2, NT])
        index = sb("index", [P, H * G], U32)
        weight = sb("weight", [P, H * G * 4])
        xa = [sb(f"xa{j}", [P, CC, BP]) for j in range(2)]
        vring = [sb(f"vring{j}", [P, ROWS, G, 2, CG]) for j in range(2)]
        carry = [sb(f"carry{j}", [P, G, CG]) for j in range(2)]
        index_now = [sb(f"index_now{j}", [P, NJ], U32) for j in range(2)]
        patch = [sb(f"patch{j}", [P, NJ, PATCH]) for j in range(2)]
        samp = [sb(f"samp{j}", [P, ROWS, C]) for j in range(2)]
        sampT = sb("sampT", [P, CC, BP])
        xr = [sb(f"xr{j}", [P, CC, BP]) for j in range(2)]
        x1T = sb("x1T", [P, ROWS, CC, P + 1])
        gram = sb("gram", [P, B, CC, P + 1])
        gram_tail = sb("gram_tail", [P, B, CC, P + 1])
        xs = [sb(f"xs{j}", [P, CC, BP]) for j in range(2)]
        bst = sb("bst", [P, CC, BLOCKS, 6])
        mv = sb("mv", [P, CC, 2])
        msq = sb("msq", [P, CC])
        mean_x = sb("mean_x", [P, CC])
        rstd_x = sb("rstd_x", [P, CC])
        pt = {n: sb("p_" + n, [P, QR, 2 * G]) for n in ("ix", "a", "b", "c", "m0", "m1")}
        pm = {n: sb("p_" + n, [P, QR, G]) for n in ("tm", "th", "w0", "w1", "ia")}

        psA = [ps(f"psA{i}") for i in range(2)]
        psI = ps("psI")
        psT = [ps(f"psT{i}") for i in range(2)]
        psO = [ps(f"psO{i}") for i in range(2)]
        psG = ps("psG")

        NU = 2 + NQ
        const_ld = sem("const_ld")
        consts = sem("consts")
        zeros = sem("zeros")
        passed = sem("passed")
        setup_v = sem("setup_v")
        st_ld = [sem(f"st_ld{j}") for j in range(2)]
        st_used = [sem(f"st_used{j}") for j in range(2)]
        st0_ld = [sem(f"st0_ld{j}") for j in range(2)]
        st0_used = [sem(f"st0_used{j}") for j in range(2)]
        st_v = sem("st_v")
        st_a = sem("st_a")
        xa_ld = [sem(f"xa_ld{j}") for j in range(2)]
        row_full = [[sem(f"row_full{j}{r}") for r in range(ROWS)] for j in range(2)]
        psA_free = [sem(f"psA_free{j}") for j in range(2)]
        v_row = sem("v_row")
        v_dup = sem("v_dup")
        v_st = [sem(f"v_st{j}") for j in range(2)]
        w_ready = sem("w_ready")
        psI_full = sem("psI_full")
        psI_free = sem("psI_free")
        place_v = sem("place_v")
        mod_in = sem("mod_in")
        mod_out = sem("mod_out")
        placed = sem("placed")
        index_cp = sem("index_cp")
        got = [[sem(f"got{j}{h}") for h in range(2)] for j in range(2)]
        weighted = sem("weighted")
        halved = sem("halved")
        sampled = [[sem(f"sampled{j}{h}") for h in range(2)] for j in range(2)]
        psT_full = [sem(f"psT_full{j}") for j in range(2)]
        psT_free = [sem(f"psT_free{j}") for j in range(2)]
        psO_full = [sem(f"psO_full{j}") for j in range(2)]
        psO_free = [sem(f"psO_free{j}") for j in range(2)]
        xr_ld = [sem(f"xr_ld{j}") for j in range(2)]
        x1_st = [sem(f"x1_st{j}") for j in range(2)]
        psG_full = [sem(f"psG_full{j}") for j in range(2)]
        psG_free = sem("psG_free")
        wh_v = sem("wh_v")
        wh_p = sem("wh_p")
        wh_a = sem("wh_a")
        ns_t = sem("ns_t")
        ns_zy = sem("ns_zy")
        ns_zt = sem("ns_zt")
        ns_new = sem("ns_new")
        map_v = sem("map_v")
        y_ld = [sem(f"y_ld{j}") for j in range(NY)]
        y_mm = [sem(f"y_mm{j}") for j in range(NY)]
        y_add = [sem(f"y_add{j}") for j in range(NY)]
        y_st = [sem(f"y_st{j}") for j in range(NY)]

        wk = patch[0][:, :, :].rearrange("p j e -> p (j e)")
        wk2 = patch[1][:, :, :].rearrange("p j e -> p (j e)")

        def area(base, at, n):
            return base[:, at:at + n]

        def alone(eng):
            eng.sem_inc(passed, 1)

        def run(eng, image, first_conv):
            image(None, None, 0)
            first_conv()
            image(None, 0, 1)
            if B > 2:
                with eng.Fori(0, B - 2) as b:
                    image(b, b + 1, b + 2)
            image(B - 2, B - 1, None)
            image(B - 1, None, None)

        def pairs(eng, pair):
            pair(0)
            with eng.Fori(1, PAIRS - 1) as i:
                pair(i)
            pair(PAIRS - 1)

        def ends(i):
            return isinstance(i, int) and i == 0, isinstance(i, int) and i == PAIRS - 1

        def conv_of(a, s, i):
            return (s, 0) if ends(i)[1] else (a, i + 1)

        NG = PAIRS + 1

        def offsets_use(b, q, more):
            if ends(q)[1]:
                return (b + 1) * NU + (3 if more else 1)
            return b * NU + 4 + q

        xs0 = [patch[j][:, :, :].rearrange("p j e -> p (j e)").rearrange("p (c n) -> p c n", c=CC)
               for j in range(2)]
        conv_bank = {False: (*psA, *psA), True: (*psA, *psO)}

        block = ctx.enter_context(nc.Block())

        gm = area(wk, 0, CC * B).rearrange("p (c b) -> p c b", b=B)
        rs = area(wk, 16, CC * B).rearrange("p (c b) -> p c b", b=B)
        sums = area(wk, 32, CC * B).rearrange("p (c b) -> p c b", b=B)
        st2 = area(wk, 48, CC * B * 2).rearrange("p (c b k) -> p c b k", b=B, k=2)
        g_b = area(wk, 80, CC * B).rearrange("p (c b) -> p c b", b=B)
        a_b = area(wk, 96, CC * B).rearrange("p (c b) -> p c b", b=B)
        d_b = area(wk, 112, CC * B).rearrange("p (c b) -> p c b", b=B)
        mu = area(wk, 128, CC)
        gmu = area(wk, 136, CC * B).rearrange("p (c b) -> p c b", b=B)
        cst = area(wk, 152, CC * B).rearrange("p (c b) -> p c b", b=B)
        tr = area(wk, 168, CC)
        rtr = area(wk, 172, CC)
        srt = area(wk, 176, CC)
        var = area(wk, 184, CC * B).rearrange("p (c b) -> p c b", b=B)
        scr = area(wk, 256, CC * B * P).rearrange("p (c b n) -> p c b n", b=B, n=P)
        cov = area(wk2, 0, CC * P).rearrange("p (c n) -> p c n", n=P)
        Y = area(wk2, 256, CC * P).rearrange("p (c n) -> p c n", n=P)
        Z = area(wk2, 512, CC * P).rearrange("p (c n) -> p c n", n=P)
        T = area(wk2, 768, CC * P).rearrange("p (c n) -> p c n", n=P)
        rowsT = area(wk2, 1024, CC * 4 * P).rearrange("p (c k n) -> p c k n", k=4, n=P)
        dg = area(wk2, 2048, CC * P).rearrange("p (c n) -> p c n", n=P)
        pw = area(wk2, 2304, CC * P).rearrange("p (c n) -> p c n", n=P)
        amap = area(wk2, 2560, CC * P).rearrange("p (c n) -> p c n", n=P)
        i15 = area(wk2, 2816, P)
        cnow = area(wk2, 2944, CC)
        y_mem = taps[:, :, :].rearrange("p r n -> p (r n)")
        y_buf = [area(y_mem, n * CC * YB, CC * YB).rearrange("p (c n) -> p c n", c=CC)
                 for n in range(NY - 2)]
        y_buf += [v[:, :, :, :, :].rearrange("p r g k e -> p (r g k e)")
                  .rearrange("p (c n) -> p c n", c=CC) for v in vring]
        y_bank = ((*psO, *psA), (*psT, psI, psG))
        mark = {}

        P_STATS = 1
        P_ROWS = P_STATS + 1
        P_GRAM = P_ROWS + CC
        P_CROSS = P_GRAM + CC * B
        P_TRACE = P_CROSS + CC
        P_PW = P_TRACE + 1
        P_CST = P_PW + CC

        @block.sync
        def _(eng):
            for dst, src in ((wA_sb[:, :, :], wA.rearrange("(c p) n -> p c n", p=P)),
                             (wO_sb[:, :, :], wO.rearrange("(c p) n -> p c n", p=P)),
                             (biasA_sb[:, :], biasA.partition_broadcast(P)),
                             (off_b[:, :], bias_off.partition_broadcast(P)),
                             (bo_sb[:, :], bias_o), (wz_sb[:, :], w_z), (bz_sb[:, :], bias_z)):
                eng.dma_start(dst, src).then_inc(const_ld, 16)
            for n, store in enumerate((*v_st, *x1_st, *y_st)):
                eng.dma_start(opening[:, n, :], bias_o).then_inc(store, 16)

            def load_s(b, i, j):
                at = eng.snap((i * 2 + j) * BP)
                p = eng.snap((b - 1) * PAIRS + i)
                eng.wait_ge(st_used[j], p + 1)
                alone(eng)
                eng.dma_start(xs[j][:, :, :], x_v[bass.ds(b, 1), :, :, bass.ds(at, BP)]
                              .rearrange("a p c n -> (a p) c n")).then_inc(st_ld[j], 16)

            def load_a(b, i, j):
                at = eng.snap((i * 2 + j) * BP)
                p = eng.snap(b * PAIRS + i)
                eng.wait_ge(row_full[j][ROWS - 1], p + 1)
                alone(eng)
                eng.dma_start(xa[j][:, :, :], x_v[bass.ds(b, 1), :, :, bass.ds(at, BP)]
                              .rearrange("a p c n -> (a p) c n")).then_inc(xa_ld[j], 16)

            def load_r(b, i, j):
                at = eng.snap((i * 2 + j) * BP)
                p = eng.snap(b * PAIRS + i)
                eng.wait_ge(psG_full[j], p + 1)
                alone(eng)
                eng.wait_ge(x1_st[j], (b * PAIRS + i) * 16 + 16)
                alone(eng)
                eng.dma_start(xr[j][:, :, :], x_v[bass.ds(b, 1), :, :, bass.ds(at, BP)]
                              .rearrange("a p c n -> (a p) c n")).then_inc(xr_ld[j], 16)

            def image(g, a, s):
                if a is None and g is None:
                    with eng.Fori(0, PIX // S0 // 2) as i:
                        for j in range(2):
                            at = eng.snap((i * 2 + j) * S0)
                            eng.wait_ge(st0_used[j], i + 1)
                            alone(eng)
                            eng.dma_start(xs0[j], x_v[s, :, :, bass.ds(at, S0)])\
                               .then_inc(st0_ld[j], 16)
                    return

                def pair(i):
                    first, last = ends(i)
                    ca, ci = conv_of(a, s, i)
                    for j in range(2):
                        if ca is not None:
                            load_a(ca, ci, j)
                        if s is not None and first and j == 0:
                            load_s(s, 0, 0)
                            load_s(s, 0, 1)
                        if g is not None:
                            load_r(g, i, j)
                        if s is not None and not last:
                            load_s(s, i + 1, j)

                pairs(eng, pair)

            def first_conv():
                for j in range(2):
                    load_a(0, 0, j)

            run(eng, image, first_conv)
            for j in range(2):
                eng.wait_ge(psG_full[j], B * PAIRS + 1)
                eng.wait_ge(x1_st[j], B * PAIRS * 16 + 16)
                eng.wait_ge(v_st[j], B * PAIRS * 16 + 16)
            with eng.Fori(0, B) as b:
                with eng.Fori(0, PIX // YB // NY) as i:
                    for j in range(NY):
                        at = eng.snap((i * NY + j) * YB)
                        eng.wait_ge(y_st[j], (b * (PIX // YB // NY) + i) * 16 + 16)
                        alone(eng)
                        eng.dma_start(y_buf[j], x1_v[bass.ds(b, 1), :, :, bass.ds(at, YB)]
                                      .rearrange("a p c n -> (a p) c n")).then_inc(y_ld[j], 16)
            for j in range(NY):
                eng.wait_ge(y_st[j], B * (PIX // YB // NY) * 16 + 16)

        @block.vector
        def _(eng):
            for row in (0, H + 1):
                eng.memset(taps[:, row, :], 0.0).then_inc(setup_v, 1)
            eng.memset(x1T[:, :, :, :], 1.0).then_inc(setup_v, 1)
            eng.memset(gram[:, :, :, :], 0.0).then_inc(setup_v, 1)
            eng.memset(carry[0][:, :, :], 0.0).then_inc(setup_v, 1)
            eng.memset(carry[1][:, :, :], 0.0).then_inc(setup_v, 1)
            eng.wait_ge(consts, 11)
            eng.wait_ge(const_ld, 16 * 7)
            eng.wait_ge(setup_v, 6)
            eng.tensor_tensor(grid[:, :, :], grid[:, :, :],
                              off_b[:, 0:2 * G].unsqueeze(1).to_broadcast([P, H, 2 * G]), ALU.add)\
               .then_inc(setup_v, 1)
            eng.tensor_scalar(first_patch[:, :, :], first_patch[:, :, :], float(W * ENT), None, ALU.mult)\
               .then_inc(setup_v, 1)
            eng.wait_ge(setup_v, 8)

            def take_stats(b, i, j):
                eng.wait_ge(st_ld[j], ((b - 1) * PAIRS + i) * 16 + 16)
                for c in range(CC):
                    ins = eng.bn_stats(bst[:, c, bass.ds(i * 2 + j, 1), :]
                                       .rearrange("p a s -> p (a s)"), xs[j][:, c, :])
                ins.then_inc(st_used[j], 1)

            NS = 7

            def prep(b):
                count = 0

                def step(ins):
                    nonlocal count
                    count += 1
                    ins.then_inc(st_v, 1)
                    eng.wait_ge(st_v, b * NS + count)

                first = isinstance(b, int) and b == 0
                for j in range(2):
                    if first:
                        eng.wait_ge(st0_used[j], PIX // S0 // 2 + 1)
                    else:
                        eng.wait_ge(st_used[j], b * PAIRS + 1)
                if not isinstance(b, int):
                    alone(eng)
                for c in range(CC):
                    agg = eng.bn_aggr(mv[:, c, :], bst[:, c, :, :].rearrange("p n s -> p (n s)"))
                step(agg)
                step(eng.tensor_tensor(msq[:, :], mv[:, :, 0], mv[:, :, 0], ALU.mult))
                step(eng.tensor_tensor(mv[:, :, 1], mv[:, :, 1], msq[:, :], ALU.add))
                eng.wait_ge(psI_full, b * NU + 1)
                pg = psI[:, 0:CC * 2].rearrange("p (c k) -> p c k", k=2)
                step(eng.tensor_copy(mean_x[:, :], pg[:, :, 0]))
                step(eng.tensor_tensor(msq[:, :], mean_x[:, :], mean_x[:, :], ALU.mult))
                eng.tensor_tensor(rstd_x[:, :], pg[:, :, 1], msq[:, :], ALU.subtract)\
                   .then_inc(psI_free, 1)
                eng.wait_ge(psI_free, b * NU + 2)
                step(eng.tensor_scalar(rstd_x[:, :], rstd_x[:, :], 0.0, EPS_GN, ALU.max, ALU.add))
                eng.wait_ge(st_a, b + 1)
                step(eng.reciprocal(rstd_x[:, :], rstd_x[:, :]))
                assert count == NS
                for c in range(CC):
                    eng.tensor_scalar(wB[:, c, :], wA_sb[:, c, :], rstd_x[:, c:c + 1],
                                      None, ALU.mult).then_inc(w_ready, 1)
                    eng.tensor_copy(mean_bc[:, c, :], mean_x[:, c:c + 1].to_broadcast([P, P]))\
                       .then_inc(w_ready, 1)
                eng.wait_ge(psI_full, b * NU + 2)
                eng.tensor_tensor(biasB[:, :], biasA_sb[:, :], psI[:, 0:NA], ALU.subtract)\
                   .then_inc(psI_free, 1)
                eng.wait_ge(psI_free, b * NU + 3)

            def conv_out(b, i, j, rows, wide):
                for r in rows:
                    k = r % 2
                    eng.wait_ge(row_full[j][r], b * PAIRS + i + 2)
                    if r == 0:
                        eng.wait_ge(v_st[j], (b * PAIRS + i) * 16 + 16)
                    if r == ROWS - 1:
                        eng.wait_ge(v_dup, (b * PAIRS + i) * 10 + 5 * j + 2)
                    dst = vring[j][:, r + 1, :, 0, :] if r < ROWS - 1 else carry[j][:, :, :]
                    bank = conv_bank[wide][r]
                    eng.tensor_tensor(dst, bank[:, 0:C].rearrange("p (g e) -> p g e", g=G),
                                      biasB[:, 0:C].rearrange("p (g e) -> p g e", g=G), ALU.add)\
                       .then_inc(v_row, 1)
                    eng.tensor_tensor(taps[:, bass.ds((i * 2 + j) * ROWS + r + 1, 1), :]
                                      .rearrange("p a n -> p (a n)"),
                                      bank[:, C:NA], biasB[:, C:NA], ALU.add)\
                       .then_inc(psA_free[k], 1)

            NV = 18

            def place(b, q, more):
                ix, a, bb, cc, m0, m1 = (pt[n][:, :, :] for n in ("ix", "a", "b", "c", "m0", "m1"))
                tm, th, w0, w1, ia = (pm[n][:, :, :] for n in ("tm", "th", "w0", "w1", "ia"))
                pq = psI[:, 0:QR * NO].rearrange("p (r o) -> p r o", o=NO)
                base = (b * NQ + q) * NV
                use = offsets_use(b, q, more)
                count = 0

                def step(ins):
                    nonlocal count
                    count += 1
                    ins.then_inc(place_v, 1)
                    return base + count

                eng.wait_ge(psI_full, use)
                eng.tensor_tensor(tm, pq[:, :, 2 * G:NO],
                                  off_b[:, 2 * G:NO].unsqueeze(1).to_broadcast([P, QR, G]),
                                  ALU.add).then_inc(mod_in, 1)
                eng.tensor_tensor(a, pq[:, :, 0:2 * G], grid[:, bass.ds(q * QR, QR), :],
                                  ALU.add).then_inc(psI_free, 1)
                eng.wait_ge(psI_free, use + 1)
                position = step(eng.tensor_scalar(ix, a, W / (W - 1.0), 0.5, ALU.mult,
                                                  ALU.subtract))
                eng.wait_ge(place_v, position)
                low = step(eng.tensor_scalar(a, ix, 0.5, 0.0, ALU.subtract, ALU.max))
                eng.wait_ge(place_v, low)
                high = step(eng.tensor_scalar(a, a, W - 2.0, MAGIC, ALU.min, ALU.add))
                eng.wait_ge(place_v, high)
                corner = step(eng.tensor_scalar(a, a, MAGIC, None, ALU.subtract))
                eng.wait_ge(place_v, corner)
                distance = step(eng.tensor_tensor(ix, ix, a, ALU.subtract))
                column = step(eng.scalar_tensor_tensor(ia, a[:, :, 0:G], float(ENT),
                                                       first_patch[:, :, :], ALU.mult, ALU.add))
                eng.wait_ge(place_v, distance)
                right = step(eng.tensor_scalar(bb, ix, -1.0, 1.0, ALU.mult, ALU.add))
                right1 = step(eng.tensor_scalar(cc, ix, -1.0, 2.0, ALU.mult, ALU.add))
                eng.wait_ge(place_v, column)
                step(eng.scalar_tensor_tensor(
                    index[:, bass.ds(q * (QR * G), QR * G)].rearrange("p (r g) -> p r g", g=G),
                    a[:, :, G:2 * G], float(VROW), ia, ALU.mult, ALU.add))
                eng.wait_ge(place_v, right)
                step(eng.scalar_tensor_tensor(m0, ix, 1.0, bb, ALU.add, ALU.min))
                eng.wait_ge(place_v, right1)
                hats = step(eng.tensor_tensor(m1, ix, cc, ALU.min))
                eng.wait_ge(mod_out, b * NQ + q + 1)
                factor = step(eng.tensor_scalar(th, th, 1.0, None, ALU.add))
                eng.wait_ge(place_v, hats)
                eng.wait_ge(place_v, factor)
                step(eng.scalar_tensor_tensor(w0, m0[:, :, G:2 * G], 0.0, th, ALU.max, ALU.mult))
                rows = step(eng.scalar_tensor_tensor(w1, m1[:, :, G:2 * G], 0.0, th, ALU.max,
                                                     ALU.mult))
                eng.wait_ge(place_v, rows)
                wv = weight[:, bass.ds(q * (QR * G * 4), QR * G * 4)]\
                    .rearrange("p (r g k) -> p r g k", g=G, k=4)
                for k, (mx, wy) in enumerate(((m0, w0), (m0, w1), (m1, w0), (m1, w1))):
                    stored = step(eng.scalar_tensor_tensor(wv[:, :, :, k], mx[:, :, 0:G], 0.0, wy,
                                                           ALU.max, ALU.mult))
                eng.wait_ge(place_v, stored)
                assert count == NV
                eng.sem_inc(placed, 1)

            def sample(b, i, j, h):
                eng.wait_ge(got[j][h], (b * PAIRS + i) * (NH * 16) + NH * 16)
                mine = patch[j][:, h * NH:(h + 1) * NH, :]
                v4 = mine.rearrange("p t (k e) -> p (t k) e", e=CG)
                w4 = weight[:, bass.ds(((i * 2 + j) * 2 + h) * (NH * 4), NH * 4)].unsqueeze(2)\
                    .to_broadcast([P, NH * 4, CG])
                eng.tensor_tensor(v4, v4, w4, ALU.mult).then_inc(weighted, 1)
                eng.wait_ge(weighted, (b * PAIRS + i) * 4 + 2 * j + h + 1)
                eng.tensor_tensor(mine[:, :, 0:ENT], mine[:, :, 0:ENT], mine[:, :, ENT:PATCH],
                                  ALU.add).then_inc(halved, 1)
                eng.wait_ge(halved, (b * PAIRS + i) * 4 + 2 * j + h + 1)
                eng.tensor_tensor(samp[j][:, 2 * h:2 * h + 2, :].rearrange("p r (g e) -> p (r g) e", g=G),
                                  mine[:, :, 0:CG], mine[:, :, CG:ENT], ALU.add)\
                   .then_inc(sampled[j][h], 1)

            def residual(b, i, j):
                eng.wait_ge(xr_ld[j], (b * PAIRS + i) * 16 + 16)
                for o in range(CC):
                    eng.wait_ge(psO_full[o], (b * PAIRS + i) * 2 + j + 2)
                    eng.scalar_tensor_tensor(xr[j][:, o, :], psO[o][:, :], bo_sb[:, o:o + 1],
                                             xr[j][:, o, :], ALU.add, ALU.add)\
                       .then_inc(psO_free[o], 1)

            def gram_add(b, i):
                eng.wait_ge(psG_full[0], b * PAIRS + i + 2)
                eng.wait_ge(psG_free, b * NG + i + 1)
                gb = gram[:, bass.ds(b, 1), :, :].rearrange("p a c n -> p (a c n)")
                eng.tensor_tensor(gb, gb, psG[:, 0:CC * (P + 1)], ALU.add).then_inc(psG_free, 1)

            def image(g, a, s):
                if a is None and g is None:
                    with eng.Fori(0, PIX // S0 // 2) as i:
                        for j in range(2):
                            eng.wait_ge(st0_ld[j], i * 16 + 16)
                            for c in range(CC):
                                for n in range(S0 // BP):
                                    at = (i * 2 + j) * (S0 // BP) + n
                                    ins = eng.bn_stats(bst[:, c, bass.ds(at, 1), :]
                                                       .rearrange("p a s -> p (a s)"),
                                                       xs0[j][:, c, n * BP:(n + 1) * BP])
                            ins.then_inc(st0_used[j], 1)
                    return

                def pair(i):
                    first, last = ends(i)
                    ca, ci = conv_of(a, s, i)
                    prepare = last and ca is not None
                    for j in range(2):
                        if g is not None:
                            sample(g, i, j, 0)
                            if j == 1:
                                residual(g, i, 0)
                            elif not first:
                                residual(g, i - 1, 1)
                                gram_add(g, i - 1)
                        if s is not None and first and j == 0:
                            take_stats(s, 0, 0)
                            take_stats(s, 0, 1)
                        if prepare and j == 0:
                            if g is not None:
                                sample(g, i, j, 1)
                            prep(ca)
                            conv_out(ca, ci, j, range(ROWS), g is None)
                            continue
                        if ca is not None:
                            conv_out(ca, ci, j, (0, 1), g is None)
                        if g is not None:
                            sample(g, i, j, 1)
                        if s is not None and not last:
                            take_stats(s, i + 1, j)
                        if ca is not None:
                            conv_out(ca, ci, j, (2, 3), g is None)
                        if a is not None and j == 1:
                            place(a, i, s is not None)

                pairs(eng, pair)
                if g is not None:
                    residual(g, PAIRS - 1, 1)
                    gram_add(g, PAIRS - 1)

            def first_conv():
                prep(0)
                eng.sem_inc(psI_free, 1)
                for j in range(2):
                    conv_out(0, 0, j, range(ROWS), True)

            run(eng, image, first_conv)

            done = 0

            def step(ins):
                nonlocal done
                done += 1
                ins.then_inc(wh_v, 1)
                eng.wait_ge(wh_v, done)

            eng.wait_ge(psG_free, B * NG + 1)
            step(eng.tensor_tensor(gram[:, :, :, :], gram[:, :, :, :], gram_tail[:, :, :, :],
                                   ALU.add))
            step(eng.tensor_copy(sums, gram[:, :, :, P:P + 1].rearrange("p b c n -> p c (b n)")))
            step(eng.tensor_scalar(st2[:, :, :, 0], sums, 1.0 / PIX, None, ALU.mult))
            for c in range(CC):
                step(eng.tensor_tensor(scr[:, c, :, :], gram[:, :, c, 0:P],
                                       ident[:, :].unsqueeze(1).to_broadcast([P, B, P]), ALU.mult))
            step(eng.tensor_reduce(var, scr, AX_X, ALU.add))
            step(eng.tensor_scalar(st2[:, :, :, 1], var, 1.0 / PIX, None, ALU.mult))
            mark["w_channels"] = done
            eng.wait_ge(wh_p, P_STATS)
            pg = psI[:, 0:CC * B * 2].rearrange("p (c b k) -> p c b k", b=B, k=2)
            step(eng.tensor_copy(gm, pg[:, :, :, 0]))
            step(eng.tensor_tensor(var, gm, gm, ALU.mult))
            step(eng.tensor_tensor(var, pg[:, :, :, 1], var, ALU.subtract))
            step(eng.tensor_scalar(var, var, 0.0, EPS_GN, ALU.max, ALU.add))
            mark["w_variance"] = done
            eng.wait_ge(wh_a, 1)
            step(eng.reciprocal(rs, var))
            step(eng.tensor_tensor(g_b, gm, rs, ALU.mult))
            step(eng.tensor_tensor(a_b, sums, rs, ALU.mult))
            step(eng.scalar_tensor_tensor(d_b, g_b, float(PIX), a_b, ALU.mult, ALU.subtract))
            step(eng.tensor_reduce(mu, d_b, AX_X, ALU.add))
            step(eng.tensor_scalar(mu, mu, -1.0 / (B * PIX), None, ALU.mult))
            for c in range(CC):
                for b in range(B):
                    step(eng.tensor_scalar(scr[:, c, b, :], gram[:, b, c, 0:P], rs[:, c, b:b + 1],
                                           None, ALU.mult))
            mark["w_scaled"] = done
            for c in range(CC):
                eng.wait_ge(wh_p, P_ROWS + c)
                step(eng.tensor_copy(rowsT[0:B, c, 0, :], psT[c][0:B, 0:P]))
                step(eng.tensor_scalar(rowsT[0:B, c, 1, :], psT[c][0:B, P:2 * P], -1.0, None, ALU.mult))
                step(eng.tensor_copy(rowsT[0:B, c, 2, :], psT[c][0:B, 2 * P:3 * P]))
                step(eng.tensor_copy(rowsT[0:1, c, 3, :], psT[c][0:1, 3 * P:4 * P]))
                step(eng.tensor_scalar(T[0:1, c, :], rowsT[0:1, c, 3, :], -float(B * PIX), None,
                                       ALU.mult))
            mark["w_rows"] = done
            for c in range(CC):
                for b in range(B):
                    n = c * B + b
                    eng.wait_ge(wh_p, P_GRAM + n)
                    if b == 0:
                        step(eng.tensor_scalar(cov[:, c, :], psA[n % 2][:, 0:P], rs[:, c, b:b + 1],
                                               None, ALU.mult))
                    else:
                        step(eng.scalar_tensor_tensor(cov[:, c, :], psA[n % 2][:, 0:P],
                                                      rs[:, c, b:b + 1], cov[:, c, :],
                                                      ALU.mult, ALU.add))
            for c in range(CC):
                eng.wait_ge(wh_p, P_CROSS + c)
                step(eng.tensor_tensor(cov[:, c, :], cov[:, c, :], psO[c][:, 0:P], ALU.add))
                step(eng.scalar_tensor_tensor(cov[:, c, :], cov[:, c, :], 1.0 / (B * PIX),
                                              same16[:, :], ALU.mult, ALU.mult))
                step(eng.scalar_tensor_tensor(cov[:, c, :], ident[:, :], EPS_Z, cov[:, c, :],
                                              ALU.mult, ALU.add))
                step(eng.tensor_tensor(Y[:, c, :], cov[:, c, :], ident[:, :], ALU.mult))
            step(eng.tensor_reduce(tr, Y, AX_X, ALU.add))
            mark["w_trace"] = done
            eng.wait_ge(wh_p, P_TRACE)
            step(eng.tensor_copy(tr, psI[:, 0:CC]))
            mark["w_root"] = done
            step(eng.reciprocal(rtr, tr))
            for c in range(CC):
                step(eng.tensor_scalar(Y[:, c, :], cov[:, c, :], rtr[:, c:c + 1], None, ALU.mult))
                step(eng.tensor_copy(Z[:, c, :], ident[:, :]))
            step(eng.tensor_scalar(i15, ident[:, :], 1.5, None, ALU.mult))
            eng.sem_inc(ns_new, 1)
            for n, f in enumerate(FACTORS):
                for c in range(CC):
                    eng.wait_ge(ns_zy, n * CC + c + 1)
                    eng.scalar_tensor_tensor(T[:, c, :], psA[c][:, 0:P], -0.5 * f * f, i15, ALU.mult,
                                             ALU.add).then_inc(ns_t, 1)
                for c in range(CC):
                    eng.wait_ge(ns_zt, n * CC + c + 1)
                    eng.tensor_scalar(Y[:, c, :], psT[c][:, 0:P], f, None, ALU.mult)
                    ins = eng.tensor_scalar(Z[:, c, :], psO[c][:, 0:P], f, None, ALU.mult)
                ins.then_inc(ns_new, 1)
            eng.wait_ge(ns_new, len(FACTORS) + 1)
            eng.wait_ge(wh_a, 2)
            step(eng.reciprocal(srt, srt))
            for c in range(CC):
                step(eng.tensor_scalar(dg[:, c, :], ident[:, :], wz_sb[:, c:c + 1], None, ALU.mult))
            mark["w_root_of_cov"] = done
            for c in range(CC):
                eng.wait_ge(wh_p, P_PW + c)
                step(eng.tensor_scalar(pw[:, c, :], psA[c][:, 0:P], srt[:, c:c + 1], None, ALU.mult))
                step(eng.tensor_scalar(gmu[:, c, :], g_b[:, c, :], mu[:, c:c + 1], None, ALU.add))
            mark["w_pw"] = done
            for c in range(CC):
                eng.wait_ge(wh_p, P_CST + CC - 1)
                step(eng.tensor_scalar(cst[:, c, :], psG[:, c * B:(c + 1) * B], -1.0,
                                       bz_sb[:, c:c + 1], ALU.mult, ALU.add))
            with eng.Fori(0, B) as b:
                for j in range(NY):
                    eng.wait_ge(y_add[j], b * (PIX // YB // NY) + 1)
                for c in range(CC):
                    eng.tensor_scalar(amap[:, c, :], pw[:, c, :], rs[:, c, bass.ds(b, 1)], None,
                                      ALU.mult).then_inc(map_v, 1)
                    eng.tensor_copy(cnow[:, c:c + 1], cst[:, c, bass.ds(b, 1)]).then_inc(map_v, 1)
                eng.wait_ge(map_v, (b + 1) * (2 * CC))
                alone(eng)
                with eng.Fori(0, PIX // YB // NY) as i:
                    for j in range(NY):
                        eng.wait_ge(y_mm[j], b * (PIX // YB // NY) + i + 1)
                        for k in range(CC * YB // 512):
                            c, at = k // (YB // 512), k % (YB // 512) * 512
                            part = y_buf[j][:, c, at:at + 512]
                            ins = eng.scalar_tensor_tensor(part, y_bank[j % 2][k][:, :],
                                                           cnow[:, c:c + 1], part, ALU.add, ALU.add)
                        ins.then_inc(y_add[j], 1)

        @block.gpsimd
        def _(eng):
            for free in (*st_used, *st0_used, *row_full[0], *row_full[1], *sampled[0], *sampled[1], *psT_free, *psO_free,
                         *psO_full, *psG_full, psG_free, *psA_free, psI_free, v_dup, *y_add):
                eng.sem_inc(free, 1)
            eng.memset(ident[:, :], 0.0).then_inc(zeros, 1)
            eng.memset(shift[:, :, :], 0.0).then_inc(zeros, 1)
            eng.memset(avg8[:, :], 1.0 / GN1).then_inc(zeros, 1)
            eng.memset(same16[:, :], 1.0).then_inc(zeros, 1)
            eng.wait_ge(zeros, 4)
            eng.affine_select(out=ident[:, :], in_=ident[:, :], compare_op=ALU.not_equal, fill=1.0,
                              base=0, pattern=[[-1, P]], channel_multiplier=1).then_inc(consts, 1)
            for d in range(3):
                eng.affine_select(out=shift[:, d, :], in_=shift[:, d, :], compare_op=ALU.not_equal,
                                  fill=1.0, base=1 - d, pattern=[[-1, P]],
                                  channel_multiplier=1).then_inc(consts, 1)
            done = 4
            for m, g in ((avg8, GN1), (same16, GZ)):
                eng.affine_select(out=m[:, :], in_=m[:, :], compare_op=ALU.is_ge, fill=0.0, base=0,
                                  pattern=[[-g, P // g], [0, g]],
                                  channel_multiplier=1).then_inc(consts, 1)
                done += 1
                eng.wait_ge(consts, done)
                eng.affine_select(out=m[:, :], in_=m[:, :], compare_op=ALU.is_ge, fill=0.0,
                                  base=g - 1, pattern=[[g, P // g], [0, g]],
                                  channel_multiplier=-1).then_inc(consts, 1)
                done += 1
            eng.iota(grid[:, :, 0:G], pattern=[[0, H], [0, G]], base=0, channel_multiplier=1,
                     allow_small_or_imprecise_dtypes=True).then_inc(consts, 1)
            eng.iota(grid[:, :, G:2 * G], pattern=[[1, H], [0, G]], base=0, channel_multiplier=0,
                     allow_small_or_imprecise_dtypes=True).then_inc(consts, 1)
            eng.iota(first_patch[:, :, :], pattern=[[0, QR], [1, G]], base=G, channel_multiplier=0,
                     allow_small_or_imprecise_dtypes=True).then_inc(consts, 1)

            def gather(b, k, i, j):
                eng.wait_ge(sampled[j][1], b * PAIRS + i + 1)
                eng.wait_ge(index_cp, (b * PAIRS + i) * 2 + j + 1)
                alone(eng)
                for t in range(NJ):
                    eng.indirect_dma_start(
                        out=patch[j][:, t, :], out_offset=None, in_=v2_flat[k],
                        in_offset=bass.IndirectOffsetOnAxis(ap=index_now[j][:, t:t + 1], axis=1),
                    ).then_inc(got[j][t // NH], 16)

            with eng.Fori(0, B // 2) as h:
                for k in range(2):
                    b = h * 2 + k
                    for j in range(2):
                        eng.wait_ge(v_st[j], (b + 1) * (PAIRS * 16) + 16)
                    alone(eng)
                    with eng.Fori(0, PAIRS) as i:
                        for j in range(2):
                            gather(b, k, i, j)

        def whiten_tensor(eng):
            eng.wait_ge(wh_v, mark["w_channels"])
            eng.matmul(psI[:, 0:CC * B * 2], avg8[:, :],
                       st2.rearrange("p c b k -> p (c b k)"), start=True, stop=True)\
               .then_inc(wh_p, 1)
            eng.wait_ge(wh_v, mark["w_scaled"])
            for c in range(CC):
                for k, m in enumerate((g_b, a_b, d_b)):
                    eng.matmul(psT[c][0:B, k * P:(k + 1) * P], m[:, c, :], ident[:, :],
                               start=True, stop=True)
                eng.matmul(psT[c][0:1, 3 * P:4 * P], mu[:, c:c + 1], ident[:, :],
                           start=True, stop=True).then_inc(wh_p, 1)
            for c in range(CC):
                for b in range(B):
                    n = c * B + b
                    if n >= 2:
                        eng.wait_ge(wh_v, mark["w_rows"] + n - 1)
                    eng.matmul(psA[n % 2][:, 0:P], scr[:, c, b, :], ident[:, :],
                               start=True, stop=True).then_inc(wh_p, 1)
            eng.wait_ge(wh_v, mark["w_rows"])
            for c in range(CC):
                eng.matmul(psO[c][:, 0:P], rowsT[0:B, c, 1, :], rowsT[0:B, c, 0, :],
                           start=True, stop=False)
                eng.matmul(psO[c][:, 0:P], rowsT[0:B, c, 0, :], rowsT[0:B, c, 2, :],
                           start=False, stop=False)
                eng.matmul(psO[c][:, 0:P], rowsT[0:1, c, 3, :], T[0:1, c, :],
                           start=False, stop=True).then_inc(wh_p, 1)
            eng.wait_ge(wh_v, mark["w_trace"])
            eng.matmul(psI[:, 0:CC], same16[:, :], tr, start=True, stop=True).then_inc(wh_p, 1)
            for n in range(len(FACTORS)):
                eng.wait_ge(ns_new, n + 1)
                for c in range(CC):
                    eng.matmul(psA[c][:, 0:P], Z[:, c, :], Y[:, c, :], start=True, stop=True)\
                       .then_inc(ns_zy, 1)
                for c in range(CC):
                    eng.wait_ge(ns_t, n * CC + c + 1)
                    eng.matmul(psT[c][:, 0:P], Y[:, c, :], T[:, c, :], start=True, stop=True)
                    eng.matmul(psO[c][:, 0:P], T[:, c, :], Z[:, c, :], start=True, stop=True)\
                       .then_inc(ns_zt, 1)
            eng.wait_ge(wh_v, mark["w_root_of_cov"])
            for c in range(CC):
                eng.matmul(psA[c][:, 0:P], Z[:, c, :], dg[:, c, :], start=True, stop=True)\
                   .then_inc(wh_p, 1)
            eng.wait_ge(wh_v, mark["w_pw"])
            for c in range(CC):
                eng.matmul(psG[:, c * B:(c + 1) * B], pw[:, c, :], gmu[:, c, :],
                           start=True, stop=True).then_inc(wh_p, 1)

        @block.tensor
        def _(eng):
            eng.wait_ge(consts, 11)
            eng.wait_ge(const_ld, 16 * 7)
            def prep(b):
                eng.wait_ge(st_v, b * 7 + 3)
                eng.wait_ge(psI_free, b * NU + 1)
                eng.matmul(psI[:, 0:CC * 2], avg8[:, :], mv[:, :, :].rearrange("p c k -> p (c k)"),
                           start=True, stop=True).then_inc(psI_full, 1)
                eng.wait_ge(w_ready, (b + 1) * 4)
                eng.wait_ge(psI_free, b * NU + 2)
                for c in range(CC):
                    mm = eng.matmul(psI[:, 0:NA], mean_bc[:, c, :], wB[:, c, :],
                                    start=(c == 0), stop=(c == CC - 1))
                mm.then_inc(psI_full, 1)

            def conv_rows(b, i, j, rows, wide):
                if 0 in rows:
                    eng.wait_ge(xa_ld[j], (b * PAIRS + i) * 16 + 16)
                for r in rows:
                    k = r % 2
                    free = (b * PAIRS + i) * 4 + 2 * j + r // 2 + (0 if wide else 1)
                    if not (isinstance(free, int) and free == 0):
                        eng.wait_ge(psA_free[k], free)
                    for c in range(CC):
                        mm = eng.matmul(conv_bank[wide][r][:, 0:NA], xa[j][:, c, r * W:(r + 1) * W],
                                        wB[:, c, :], start=(c == 0), stop=(c == CC - 1))
                    mm.then_inc(row_full[j][r], 1)

            def offsets(b, q, more):
                for k in range(2):
                    eng.wait_ge(psA_free[k], (b * PAIRS + q) * 4 + 5 + (0 if ends(q)[1] else 2))
                eng.wait_ge(psI_free, offsets_use(b, q, more))
                for t in range(NTAP):
                    dy, dx = t // 3, t % 3
                    mm = eng.matmul(psI[:, 0:QR * NO].rearrange("p (r o) -> p r o", o=NO),
                                    shift[:, dx, :],
                                    taps[:, bass.ds(q * QR + dy, QR), t * NO:(t + 1) * NO],
                                    start=(t == 0), stop=(t == NTAP - 1))
                mm.then_inc(psI_full, 1)

            def turn_samples(b, i, j, h):
                eng.wait_ge(sampled[j][h], b * PAIRS + i + 2)
                for c in range(CC):
                    if h == 0:
                        eng.wait_ge(psT_free[c], (b * PAIRS + i) * 4 + 2 * j + 1)
                    for r in (2 * h, 2 * h + 1):
                        mm = eng.transpose(psT[c][:, r * W:(r + 1) * W],
                                           samp[j][:, r, c * P:(c + 1) * P], ident[:, :])
                    if h == 1:
                        mm.then_inc(psT_full[c], 1)

            def out_conv(b, i, j):
                for h in range(CC):
                    eng.wait_ge(psT_free[h], (b * PAIRS + i) * 4 + 2 * j + 2)
                for o in range(CC):
                    eng.wait_ge(psO_free[o], (b * PAIRS + i) * 2 + j + 1)
                    for h in range(CC):
                        mm = eng.matmul(psO[o][:, :], wO_sb[:, h, o * P:(o + 1) * P],
                                        sampT[:, h, :], start=(h == 0), stop=(h == CC - 1))
                    mm.then_inc(psO_full[o], 1)

            def turn_x1(b, i, j):
                for o in range(CC):
                    eng.wait_ge(psO_free[o], (b * PAIRS + i) * 2 + j + 2)
                for h in range(2):
                    eng.wait_ge(psT_free[h], (b * PAIRS + i) * 4 + 2 * j + 2)
                    for r in range(2):
                        for c in range(CC):
                            at = (r * CC + c) * P
                            row = 2 * h + r
                            mm = eng.transpose(psT[h][:, at:at + P],
                                               xr[j][:, c, row * W:(row + 1) * W], ident[:, :])
                    mm.then_inc(psT_full[h], 1)

            def gram_block(b, i, j):
                first, last = ends(i)[0] and j == 0, ends(i)[1] and j == 1
                opens, closes = j == 1 or first, j == 0 or last
                for h in range(2):
                    eng.wait_ge(psT_free[h], (b * PAIRS + i) * 4 + 2 * j + 3)
                if opens:
                    eng.wait_ge(psG_free, b * NG + (1 if first else i + 2))
                for c in range(CC):
                    for r in range(ROWS):
                        mm = eng.matmul(psG[:, c * (P + 1):(c + 1) * (P + 1)], x1T[:, r, c, 0:P],
                                        x1T[:, r, c, :], start=(opens and c == 0 and r == 0),
                                        stop=(closes and c == CC - 1 and r == ROWS - 1))
                mm.then_inc(psG_full[j], 1)

            def image(g, a, s):
                if a is None and g is None:
                    return

                def pair(i):
                    first, last = ends(i)
                    ca, ci = conv_of(a, s, i)
                    prepare = last and ca is not None
                    for j in range(2):
                        def conv(rows):
                            if ca is not None:
                                conv_rows(ca, ci, j, rows, g is None)

                        def before(part):
                            if j == 1:
                                part(g, i, 0)
                            elif not first:
                                part(g, i - 1, 1)

                        if g is None:
                            if prepare and j == 0:
                                prep(ca)
                            conv(range(ROWS))
                            if j == 1:
                                offsets(a, i, s is not None)
                        elif prepare and j == 0:
                            before(out_conv)
                            before(turn_x1)
                            turn_samples(g, i, j, 0)
                            before(gram_block)
                            turn_samples(g, i, j, 1)
                            prep(ca)
                            conv(range(ROWS))
                        else:
                            conv((0, 1))
                            before(out_conv)
                            before(turn_x1)
                            conv((2,))
                            if a is not None and j == 1:
                                offsets(a, i, s is not None)
                            turn_samples(g, i, j, 0)
                            conv((3,))
                            turn_samples(g, i, j, 1)
                            before(gram_block)

                pairs(eng, pair)
                if g is not None:
                    out_conv(g, PAIRS - 1, 1)
                    turn_x1(g, PAIRS - 1, 1)
                    gram_block(g, PAIRS - 1, 1)

            def first_conv():
                prep(0)
                eng.wait_ge(psI_free, 3)
                eng.sem_inc(psI_full, 1)
                for j in range(2):
                    conv_rows(0, 0, j, range(ROWS), True)

            run(eng, image, first_conv)
            whiten_tensor(eng)
            with eng.Fori(0, B) as b:
                eng.wait_ge(map_v, (b + 1) * (2 * CC))
                alone(eng)
                with eng.Fori(0, PIX // YB // NY) as i:
                    for j in range(NY):
                        eng.wait_ge(y_ld[j], (b * (PIX // YB // NY) + i) * 16 + 16)
                        if j < 2:
                            eng.wait_ge(y_add[j + NY - 2], b * (PIX // YB // NY) + i + 1)
                        else:
                            eng.wait_ge(y_add[j - 2], b * (PIX // YB // NY) + i + 2)
                        for k in range(CC * YB // 512):
                            c, at = k // (YB // 512), k % (YB // 512) * 512
                            mm = eng.matmul(y_bank[j % 2][k][:, :], amap[:, c, :],
                                            y_buf[j][:, c, at:at + 512], start=True, stop=True)
                        mm.then_inc(y_mm[j], 1)

        @block.scalar
        def _(eng):
            def root(b):
                eng.wait_ge(st_v, b * 7 + 6)
                eng.activation(rstd_x[:, :], rstd_x[:, :], ACT.Sqrt).then_inc(st_a, 1)

            def dup(b, i, j, rows):
                for r in rows:
                    src = vring[j][:, r + 1, :, 0, :] if r < ROWS - 1 else carry[j][:, :, :]
                    eng.wait_ge(v_row, (b * PAIRS + i) * 8 + 4 * j + r + 1)
                    if r == 0:
                        eng.activation(vring[j][:, 0, :, 0, :], carry[1 - j][:, :, :], ACT.Copy)\
                           .then_inc(v_dup, 1)
                    eng.activation(vring[j][:, r, :, 1, :], src, ACT.Copy).then_inc(v_dup, 1)

            def v_store(b, k, i, j):
                row = eng.snap((i * 2 + j) * NJ)
                eng.wait_ge(v_dup, (b * PAIRS + i) * 10 + 5 * j + 6)
                eng.dma_start(v2_rows[k][:, bass.ds(row, NJ), :],
                              vring[j][:, :, :, :, :].rearrange("p r g k e -> p (r g) (k e)"))\
                   .then_inc(v_st[j], 16)

            def samples_out(b, i, j):
                eng.wait_ge(psO_full[CC - 1], (b * PAIRS + i) * 2 + j + 1)
                for h in range(CC):
                    eng.wait_ge(psT_full[h], (b * PAIRS + i) * 4 + 2 * j + 1)
                    eng.activation(sampT[:, h, :], psT[h][:, :], ACT.Copy).then_inc(psT_free[h], 1)

            def x1_store(b, i, j):
                at = eng.snap((i * 2 + j) * BP)
                bb = eng.snap(b) if not isinstance(b, int) else b
                for o in range(CC):
                    eng.wait_ge(psO_free[o], (b * PAIRS + i) * 2 + j + 2)
                eng.dma_start(x1_v[bass.ds(bb, 1), :, :, bass.ds(at, BP)]
                              .rearrange("a p c n -> (a p) c n"), xr[j][:, :, :])\
                   .then_inc(x1_st[j], 16)

            def x1_out(b, i, j):
                eng.wait_ge(psG_full[1 - j], b * PAIRS + i + j + 1)
                for h in range(2):
                    eng.wait_ge(psT_full[h], (b * PAIRS + i) * 4 + 2 * j + 2)
                    eng.activation(x1T[:, 2 * h:2 * h + 2, :, 0:P].rearrange("p r c n -> p (r c) n"),
                                   psT[h][:, :].rearrange("p (q n) -> p q n", n=P), ACT.Copy)\
                       .then_inc(psT_free[h], 1)

            def gram_out(b):
                eng.wait_ge(psG_full[1], (b + 1) * PAIRS + 1)
                eng.activation(gram_tail[:, bass.ds(b, 1), :, :].rearrange("p a c n -> p (a c n)"),
                               psG[:, 0:CC * (P + 1)], ACT.Copy).then_inc(psG_free, 1)

            def indices(b, i, j):
                eng.wait_ge(sampled[j][1], b * PAIRS + i + 1)
                eng.wait_ge(placed, b * NQ + i + 1)
                eng.activation(index_now[j][:, :], index[:, bass.ds((i * 2 + j) * NJ, NJ)], ACT.Copy)\
                   .then_inc(index_cp, 1)

            def modulation(b, q):
                eng.wait_ge(mod_in, b * NQ + q + 1)
                eng.activation(pm["th"][:, :, :], pm["tm"][:, :, :], ACT.Tanh).then_inc(mod_out, 1)

            def image(g, a, s, k):
                def pair(i):
                    first, last = ends(i)
                    ca, ci = conv_of(a, s, i)
                    prepare = last and ca is not None
                    for j in range(2):
                        if g is not None:
                            if j == 1:
                                x1_store(g, i, 0)
                                x1_out(g, i, 0)
                            elif not first:
                                x1_store(g, i - 1, 1)
                                x1_out(g, i - 1, 1)
                        if ca is not None and not (prepare and j == 0):
                            dup(ca, ci, j, (0, 1))
                        if g is not None:
                            samples_out(g, i, j)
                        if not last:
                            if g is not None:
                                indices(g, i + 1, j)
                        elif a is not None:
                            indices(a, 0, j)
                        if prepare and j == 0:
                            root(ca)
                            dup(ca, ci, j, (0, 1))
                        if ca is not None:
                            dup(ca, ci, j, (2, 3))
                            if not last:
                                v_store(ca, k, ci, j)
                            elif j == 1:
                                v_store(ca, 1 - k, ci, 0)
                                v_store(ca, 1 - k, ci, 1)
                        if a is not None and j == 1:
                            modulation(a, i)

                pairs(eng, pair)
                if g is not None:
                    x1_store(g, PAIRS - 1, 1)
                    x1_out(g, PAIRS - 1, 1)
                    gram_out(g)

            root(0)
            for j in range(2):
                dup(0, 0, j, range(ROWS))
                v_store(0, 0, 0, j)
            image(None, 0, 1, 0)
            if B > 2:
                with eng.Fori(0, B // 2 - 1) as h:
                    for k in range(2):
                        image(h * 2 + k, h * 2 + k + 1, h * 2 + k + 2, 1 - k)
            image(B - 2, B - 1, None, 1)
            image(B - 1, None, None, None)
            eng.wait_ge(wh_v, mark["w_variance"])
            eng.activation(var, var, ACT.Sqrt).then_inc(wh_a, 1)
            eng.wait_ge(wh_v, mark["w_root"])
            eng.activation(srt, tr, ACT.Sqrt).then_inc(wh_a, 1)
            with eng.Fori(0, B) as b:
                with eng.Fori(0, PIX // YB // NY) as i:
                    for j in range(NY):
                        at = eng.snap((i * NY + j) * YB)
                        eng.wait_ge(y_add[j], b * (PIX // YB // NY) + i + 2)
                        eng.dma_start(out_v[bass.ds(b, 1), :, :, bass.ds(at, YB)]
                                      .rearrange("a p c n -> (a p) c n"), y_buf[j])\
                           .then_inc(y_st[j], 16)


def kernel(x, L0_conv_offset_w, L0_conv_offset_b, L0_conv_mod_w, L0_conv_mod_b, L0_conv_kv_w,
           L0_conv_kv_b, L0_conv_out_w, L0_conv_out_b, L1_conv_weight, L1_conv_bias):
    import numpy as np
    import concourse.bacc as bacc
    from concourse.bass_utils import run_bass_kernel_spmd

    arr = lambda a: np.ascontiguousarray(a)
    B = x.shape[0]
    heads = C // 32
    perm = np.arange(C).reshape(heads // G, G, 32).transpose(1, 0, 2).reshape(-1)
    order = np.arange(2 * G).reshape(G, 2).T.reshape(-1)
    kv_w = np.asarray(L0_conv_kv_w)[C:, :, 0, 0][perm]
    kv_b = np.asarray(L0_conv_kv_b)[C:][perm]
    taps = np.concatenate([np.asarray(L0_conv_offset_w)[order], np.asarray(L0_conv_mod_w)])
    off_b = np.concatenate([np.asarray(L0_conv_offset_b)[order], np.asarray(L0_conv_mod_b)])
    arrays = {
        "x_dram": arr(x),
        "wA_dram": arr(np.concatenate([kv_w.T, taps.transpose(1, 2, 3, 0).reshape(C, NT)], 1)),
        "biasA_dram": arr(np.concatenate([kv_b, np.zeros(NT, kv_b.dtype)])),
        "bias_off_dram": arr(off_b),
        "wO_dram": arr(np.asarray(L0_conv_out_w)[:, :, 0, 0].T[perm]),
        "bias_o_dram": arr(np.asarray(L0_conv_out_b).reshape(CC, P).T),
        "w_z_dram": arr(np.asarray(L1_conv_weight).reshape(CC, P).T),
        "bias_z_dram": arr(np.asarray(L1_conv_bias).reshape(CC, P).T),
    }
    nc = bacc.Bacc("TRN2", target_bir_lowering=False, num_devices=1)
    args = [nc.dram_tensor(n, a.shape, mybir.dt.from_np(a.dtype), kind="ExternalInput").ap()
            for n, a in arrays.items()]
    out = nc.dram_tensor("out_dram", x.shape, F32, kind="ExternalOutput").ap()
    deform_zca_kernel(nc, B, *args, out)
    r = run_bass_kernel_spmd(nc, [arrays], core_ids=[0])
    return r.results[0]["out_dram"]
```
